# Optimizing a Trainium2 kernel written in Bass

```python
import numpy as np
import jax
import jax.numpy as jnp

def _softmax(x, axis=-1):
    return jax.nn.softmax(x, axis=axis)

def _gelu(x):
    return jax.nn.gelu(x, approximate=True)

def _silu(x):
    return jax.nn.silu(x)

def _sigmoid(x):
    return jax.nn.sigmoid(x)

def _layernorm(x, axis=-1, eps=1e-05):
    m = jnp.mean(x, axis=axis, keepdims=True)
    v = jnp.var(x, axis=axis, keepdims=True)
    return (x - m) / jnp.sqrt(v + eps)

def _scatter_add(tgt, idx, src, axis=0):
    return tgt.at[idx].add(src)

def _segment_sum(src, seg, n):
    return jax.ops.segment_sum(src, seg, n)
kernel_name = 'mk_adj_resnorm_d1_adj_r2_4501f5'

def setup_inputs(seed: int=0):
    np.random.seed(seed)
    _w = jnp.asarray

    def _rec_inputs():
        import jax
        import jax.numpy as jnp
        _gk = jax.random.key(seed)
        x = -9.806e-05 + 1 * jax.random.normal(jax.random.fold_in(_gk, 1), (8192, 128), jnp.float32)
        _w = (1.0 + jnp.arange(8192, dtype=jnp.float32)) ** (-0.5)
        _w = _w / _w.mean()
        _pij = jnp.clip(0.00195312 * _w[:, None] * _w[None, :], 0.0, 1.0)
        _a = jax.random.uniform(jax.random.fold_in(_gk, 2), (8192, 8192)) < _pij
        _af = _a.astype(jnp.float32)
        adj = _af
        return (x, adj)
    x, adj = _rec_inputs()

    def _L0_gnn_setup():
        import jax, jax.numpy as jnp
        import numpy as np
        N, IN, H, C = (2048, 128, 4, 32)
        HC = H * C
        EDGE_P = 0.008

        def _linear_params(key, fan_in, fan_out, bias=True):
            k1, k2 = jax.random.split(key)
            lim = 1.0 / np.sqrt(fan_in)
            W = jax.random.uniform(k1, (fan_in, fan_out), jnp.float32, -lim, lim)
            if not bias:
                return W
            b = jax.random.uniform(k2, (fan_out,), jnp.float32, -lim, lim)
            return (W, b)

        def _transformer_conv(x, adj, Wq, bq, Wk, bk, Wv, bv, Ws, bs, Wb):
            n = x.shape[0]
            q = (x @ Wq + bq).reshape(n, H, C)
            k = (x @ Wk + bk).reshape(n, H, C)
            v = (x @ Wv + bv).reshape(n, H, C)
            attn = jnp.einsum('nhc,mhc->hnm', q, k) / np.float32(np.sqrt(C))
            mask = adj == 0.0
            neg = jnp.where(mask[None], -jnp.inf, attn)
            m = jnp.max(neg, axis=-1, keepdims=True)
            all_inf = jnp.isneginf(m)
            e = jnp.where(mask[None], 0.0, jnp.exp(neg - jnp.where(all_inf, 0.0, m)))
            denom = jnp.sum(e, axis=-1, keepdims=True)
            alpha = e / jnp.where(denom == 0.0, 1.0, denom)
            out = jnp.einsum('hnm,mhc->hnc', alpha, v)
            out = jnp.transpose(out, (1, 2, 0)).reshape(n, C * H)
            x_r = x @ Ws + bs
            beta = jax.nn.sigmoid(jnp.concatenate([out, x_r, out - x_r], axis=-1) @ Wb)
            return beta * x_r + (1.0 - beta) * out
        key = jax.random.key(seed)
        ks = jax.random.split(key, 7)
        x = jax.random.normal(ks[0], (N, IN), jnp.float32)
        adj = (jax.random.uniform(ks[1], (N, N)) < EDGE_P).astype(jnp.float32)
        Wq, bq = _linear_params(ks[2], IN, HC)
        Wk, bk = _linear_params(ks[3], IN, HC)
        Wv, bv = _linear_params(ks[4], IN, HC)
        Ws, bs = _linear_params(ks[5], IN, HC)
        Wb = _linear_params(ks[6], 3 * HC, 1, bias=False)
        return dict(x=x, adj=adj, Wq=Wq, bq=bq, Wk=Wk, bk=bk, Wv=Wv, bv=bv, Ws=Ws, bs=bs, Wb=Wb)
    _L0_gnn_all = _L0_gnn_setup()
    _L0_gnn_in = {k: v for k, v in _L0_gnn_all.items() if k in ('Wq', 'bq', 'Wk', 'bk', 'Wv', 'bv', 'Ws', 'bs', 'Wb')}
    del _L0_gnn_all
    return {'x': x, 'adj': adj, 'L0_gnn_Wq': _L0_gnn_in['Wq'], 'L0_gnn_bq': _L0_gnn_in['bq'], 'L0_gnn_Wk': _L0_gnn_in['Wk'], 'L0_gnn_bk': _L0_gnn_in['bk'], 'L0_gnn_Wv': _L0_gnn_in['Wv'], 'L0_gnn_bv': _L0_gnn_in['bv'], 'L0_gnn_Ws': _L0_gnn_in['Ws'], 'L0_gnn_bs': _L0_gnn_in['bs'], 'L0_gnn_Wb': _L0_gnn_in['Wb']}

def reference(x, adj, L0_gnn_Wq, L0_gnn_bq, L0_gnn_Wk, L0_gnn_bk, L0_gnn_Wv, L0_gnn_bv, L0_gnn_Ws, L0_gnn_bs, L0_gnn_Wb):
    import jax
    import jax.numpy as jnp

    def _L0_gnn_ref(x, adj, Wq, bq, Wk, bk, Wv, bv, Ws, bs, Wb):
        import jax, jax.numpy as jnp
        import numpy as np
        N, IN, H, C = (2048, 128, 4, 32)
        HC = H * C
        EDGE_P = 0.008

        def _linear_params(key, fan_in, fan_out, bias=True):
            k1, k2 = jax.random.split(key)
            lim = 1.0 / np.sqrt(fan_in)
            W = jax.random.uniform(k1, (fan_in, fan_out), jnp.float32, -lim, lim)
            if not bias:
                return W
            b = jax.random.uniform(k2, (fan_out,), jnp.float32, -lim, lim)
            return (W, b)

        def _transformer_conv(x, adj, Wq, bq, Wk, bk, Wv, bv, Ws, bs, Wb):
            n = x.shape[0]
            q = (x @ Wq + bq).reshape(n, H, C)
            k = (x @ Wk + bk).reshape(n, H, C)
            v = (x @ Wv + bv).reshape(n, H, C)
            attn = jnp.einsum('nhc,mhc->hnm', q, k) / np.float32(np.sqrt(C))
            mask = adj == 0.0
            neg = jnp.where(mask[None], -jnp.inf, attn)
            m = jnp.max(neg, axis=-1, keepdims=True)
            all_inf = jnp.isneginf(m)
            e = jnp.where(mask[None], 0.0, jnp.exp(neg - jnp.where(all_inf, 0.0, m)))
            denom = jnp.sum(e, axis=-1, keepdims=True)
            alpha = e / jnp.where(denom == 0.0, 1.0, denom)
            out = jnp.einsum('hnm,mhc->hnc', alpha, v)
            out = jnp.transpose(out, (1, 2, 0)).reshape(n, C * H)
            x_r = x @ Ws + bs
            beta = jax.nn.sigmoid(jnp.concatenate([out, x_r, out - x_r], axis=-1) @ Wb)
            return beta * x_r + (1.0 - beta) * out
        return _transformer_conv(x, adj, Wq, bq, Wk, bk, Wv, bv, Ws, bs, Wb)
    x = _layernorm(x + _L0_gnn_ref(x, adj, L0_gnn_Wq, L0_gnn_bq, L0_gnn_Wk, L0_gnn_bk, L0_gnn_Wv, L0_gnn_bv, L0_gnn_Ws, L0_gnn_bs, L0_gnn_Wb), axis=-1)
    return x

_drawn_inputs = setup_inputs


def setup_inputs(seed=0):
    import zlib

    import numpy as np

    out = dict(_drawn_inputs(seed))
    spreads = {}
    factors = {'L0_gnn_bq': 21.456, 'L0_gnn_bk': 64.0}
    for name, (base, spread) in spreads.items():
        noise = np.random.default_rng([zlib.crc32(name.encode()), seed]).standard_normal(out[name].shape)
        drawn = base * np.exp(spread * noise) if base else spread * noise
        out[name] = jnp.asarray(drawn.astype(out[name].dtype))
    for name, factor in factors.items():
        out[name] = (out[name] * factor).astype(out[name].dtype)
    return out
```

```python
import concourse.bass as bass
from concourse import mybir
from contextlib import ExitStack

F32 = mybir.dt.float32
BF16 = mybir.dt.bfloat16
U16 = mybir.dt.uint16
U32 = mybir.dt.uint32
I32 = mybir.dt.int32
ALU = mybir.AluOpType
ACT = mybir.ActivationFunctionType
AX = mybir.AxisListType.X

P = 128
N = 8192
D = 128
H, C = 4, 32
T = N // P
SCALE = float(C) ** -0.5
EPS = 1e-5
MASKED = -1e30
FLOOR = -1e29
GROUP = 4


def gnn_resnorm_kernel(nc, x, adj, Wq, bq, Wk, bk, Wv, bv, Ws, bs, Wb, out):
    outer = ExitStack()
    with outer:
        kv_dram = nc.dram_tensor("kv_rows", (N, 2 * D), F32, kind="Internal").ap()
        qr_dram = nc.dram_tensor("qr_rows", (N, 2 * D), F32, kind="Internal").ap()
        kt_dram = nc.dram_tensor("k_columns", (D, N), F32, kind="Internal").ap()

        def keep(name, shape, dt):
            return outer.enter_context(nc.sbuf_tensor(name, shape, dt))

        ident = keep("ident", [P, P], F32)
        gate_w = keep("gate_w", [P, 2 * D], F32)
        eps_col = keep("eps_col", [P, 1], F32)
        tile_list = keep("tile_list", [1, T], I32)
        n_dense = keep("n_dense", [1, 1], I32)

        project_nodes(nc, x, Wq, bq, Wk, bk, Wv, bv, Ws, bs, Wb, kv_dram, qr_dram, kt_dram,
                      ident, gate_w, eps_col, tile_list, n_dense)
        dense_tiles(nc, x, adj, kv_dram, qr_dram, kt_dram, ident, gate_w, eps_col, tile_list, n_dense, out)


def project_nodes(nc, x, Wq, bq, Wk, bk, Wv, bv, Ws, bs, Wb, kv_dram, qr_dram, kt_dram,
                  ident, gate_w, eps_col, tile_list, n_dense):
    ctx = ExitStack()
    with ctx:
        def sb(name, shape, dt):
            return ctx.enter_context(nc.sbuf_tensor(name, shape, dt))

        def ps(name, shape, dt):
            return ctx.enter_context(nc.psum_tensor(name, shape, dt))

        def sem(name):
            return ctx.enter_context(nc.semaphore(name))

        w_all = sb("w_all", [P, 4 * D], F32)
        b_row = sb("b_row", [1, 4 * D], F32)
        b_all = sb("b_all", [P, 4 * D], F32)
        bk_col = sb("bk_col", [P, 1], F32)
        wb_row = sb("wb_row", [1, 3 * D], F32)
        gw_row = sb("gw_row", [1, 2 * D], F32)
        ones = sb("ones", [1, P], F32)
        x_in = sb("x_in", [P, 2, GROUP, D], F32)
        xT = sb("xT", [P, 2, GROUP * P], F32)
        rows = sb("rows", [P, 2, GROUP, 4 * D], F32)
        kT = sb("kT", [P, 2, GROUP * P], F32)
        ps_t = [ps(f"ps_t{i}", [P, GROUP * P], F32) for i in range(2)]
        ps_r = [ps(f"ps_r{i}", [P, 4 * D], F32) for i in range(4)]
        ps_k = [ps(f"ps_k{i}", [P, GROUP * P], F32) for i in range(2)]

        weights_in = sem("weights_in")
        x_loaded = [sem(f"x_loaded{i}") for i in range(2)]
        const_ready = sem("const_ready")
        bias_spread = sem("bias_spread")
        bias_ready = sem("bias_ready")
        x_turned = sem("x_turned")
        xT_ready = sem("xT_ready")
        rows_summed = sem("rows_summed")
        rows_ready = sem("rows_ready")
        kT_summed = sem("kT_summed")
        kT_ready = sem("kT_ready")
        stored = [sem(f"stored{i}") for i in range(2)]
        sp_turn = sem("sp_turn")

        def node_rows(a, row):
            return a[bass.ds(row, GROUP * P), :].rearrange("(j p) c -> p j c", p=P)

        block = ctx.enter_context(nc.Block())

        @block.sync
        def _(sp):
            for k, w in enumerate((Wk, Wv, Wq, Ws)):
                sp.dma_start(w_all[:, k * D:(k + 1) * D], w).then_inc(weights_in, 16)
            for k, b in enumerate((bk, bv, bq, bs)):
                sp.dma_start(b_row[0:1, k * D:(k + 1) * D], b.rearrange("(a c) -> a c", a=1)).then_inc(weights_in, 16)
            sp.dma_start(bk_col[:], bk.rearrange("(c a) -> c a", a=1)).then_inc(weights_in, 16)
            sp.dma_start(wb_row[:], Wb.rearrange("c a -> a c")).then_inc(weights_in, 16)
            for g in range(2):
                sp.dma_start(x_in[:, g], node_rows(x, g * GROUP * P)).then_inc(x_loaded[g], 16)
            with sp.Fori(0, T // GROUP // 2) as i:
                for g in range(2):
                    row = sp.snap((2 * i + g) * (GROUP * P))
                    ahead = sp.snap(((2 * i + g + 2) % (T // GROUP)) * (GROUP * P))
                    sp.wait_ge(rows_ready, GROUP * (2 * i + g + 2))
                    sp.dma_start(node_rows(kv_dram, row), rows[:, g, :, 0:2 * D]).then_inc(stored[g], 16)
                    sp.dma_start(node_rows(qr_dram, row), rows[:, g, :, 2 * D:4 * D]).then_inc(stored[g], 16)
                    sp.wait_ge(kT_ready, 2 * i + g + 1)
                    sp.sem_inc(sp_turn, 1)
                    sp.dma_start(kt_dram[:, bass.ds(row, GROUP * P)], kT[:, g]).then_inc(stored[g], 16)
                    sp.dma_start(x_in[:, g], node_rows(x, ahead)).then_inc(x_loaded[g], 16)
            for g in range(2):
                sp.wait_ge(stored[g], 48 * (T // GROUP // 2))
                sp.wait_ge(x_loaded[g], 16 * (T // GROUP // 2 + 1))

        @block.gpsimd
        def _(pool):
            nc.gpsimd.memset(ones[:], 1.0).then_inc(const_ready, 1)
            nc.gpsimd.memset(eps_col[:], EPS).then_inc(const_ready, 1)
            nc.gpsimd.memset(n_dense[:], T).then_inc(const_ready, 1)
            nc.gpsimd.iota(tile_list[:], pattern=[[1, T]], base=0, channel_multiplier=0).then_inc(const_ready, 1)
            nc.gpsimd.memset(ident[:], 0.0).then_inc(const_ready, 1)
            pool.wait_ge(const_ready, 5)
            nc.gpsimd.affine_select(out=ident[:], in_=ident[:], compare_op=ALU.not_equal, fill=1.0, base=0,
                                    pattern=[[-1, P]], channel_multiplier=1).then_inc(const_ready, 1)

        @block.tensor
        def _(pe):
            pe.wait_ge(weights_in, 160)
            pe.wait_ge(const_ready, 6)
            pe.wait_ge(bias_spread, 1)
            nc.tensor.matmul(ps_r[0][:], ones[:], b_row[:], start=True, stop=True)
            nc.tensor.matmul(ps_r[1][:, 0:2 * D], ones[:], gw_row[:], start=True, stop=True).then_inc(rows_summed, 1)
            pe.wait_ge(bias_ready, 1)
            with pe.Fori(0, T // GROUP // 2) as i:
                for g in range(2):
                    grp = 2 * i + g
                    pe.wait_ge(x_loaded[g], 16 * i + 16)
                    for j in range(GROUP):
                        last = nc.tensor.transpose(ps_t[g][:, j * P:(j + 1) * P], x_in[:, g, j], ident[:])
                    last.then_inc(x_turned, 1)
                    pe.wait_ge(xT_ready, grp + 1)
                    nc.tensor.matmul(ps_k[g][:], w_all[:, 0:D], xT[:, g], start=True, stop=True).then_inc(kT_summed, 1)
                    for j in range(GROUP):
                        pe.wait_ge(rows_ready, GROUP * grp + j + 1)
                        nc.tensor.matmul(ps_r[j][:], xT[:, g, j * P:(j + 1) * P], w_all[:], start=True,
                                         stop=True).then_inc(rows_summed, 1)

        @block.scalar
        def _(act):
            act.wait_ge(weights_in, 160)
            with act.Fori(0, T // GROUP // 2) as i:
                for g in range(2):
                    grp = 2 * i + g
                    act.wait_ge(x_turned, grp + 1)
                    nc.scalar.copy(xT[:, g], ps_t[g][:]).then_inc(xT_ready, 1)
                    act.wait_ge(stored[g], 48 * i)
                    act.wait_ge(kT_summed, grp + 1)
                    nc.scalar.activation(kT[:, g], ps_k[g][:], ACT.Identity, bias=bk_col[:]).then_inc(kT_ready, 1)

        @block.vector
        def _(dve):
            dve.wait_ge(weights_in, 160)
            nc.vector.tensor_tensor(gw_row[0:1, 0:D], wb_row[0:1, 0:D], wb_row[0:1, 2 * D:3 * D], ALU.add)
            nc.vector.tensor_tensor(gw_row[0:1, D:2 * D], wb_row[0:1, D:2 * D], wb_row[0:1, 2 * D:3 * D],
                                    ALU.subtract).then_inc(bias_spread, 1)
            dve.wait_ge(rows_summed, 1)
            nc.vector.tensor_copy(b_all[:], ps_r[0][:])
            nc.vector.tensor_copy(gate_w[:], ps_r[1][:, 0:2 * D]).then_inc(bias_ready, 1)
            dve.drain()
            dve.sem_inc(rows_ready, GROUP)
            with dve.Fori(0, T // GROUP // 2) as i:
                for g in range(2):
                    dve.wait_ge(stored[g], 48 * i)
                    for j in range(GROUP):
                        dve.wait_ge(rows_summed, 4 * (2 * i + g) + j + 2)
                        nc.vector.tensor_tensor(rows[:, g, j], ps_r[j][:], b_all[:], ALU.add).then_inc(rows_ready, 1)


def dense_tiles(nc, x, adj, kv_dram, qr_dram, kt_dram, ident, gate_w, eps_col, tile_list, n_dense, out):
    SW = 1024
    SG = N // SW
    EW = 2048
    TW = 512
    TG = N // TW
    ctx = ExitStack()
    with ctx:
        def sb(name, shape, dt):
            return ctx.enter_context(nc.sbuf_tensor(name, shape, dt))

        def ps(name, shape, dt):
            return ctx.enter_context(nc.psum_tensor(name, shape, dt))

        def sem(name):
            return ctx.enter_context(nc.semaphore("d_" + name))

        kT = sb("d_kT", [P, N], F32)
        v_rows = sb("d_v", [P, T, D], F32)
        adj_in = sb("d_adj", [P, N], F32)
        pen = sb("d_pen", [P, N], BF16)
        sc = sb("d_sc", [P, 2, N], F32)
        q_in = sb("d_q", [P, D], F32)
        qT = sb("d_qT", [P, P], F32)
        o_r = sb("d_or", [P, 2 * D], F32)
        x_in = sb("d_x", [P, D], F32)
        wT = sb("d_wT", [P, 2, TW], F32)
        gmax = sb("d_gmax", [P, H, SG], F32)
        shift = sb("d_shift", [P, H], F32)
        dsum = sb("d_dsum", [P, H, N // EW], F32)
        den = sb("d_den", [P, H], F32)
        isz = sb("d_isz", [P, H], F32)
        rden = sb("d_rden", [P, H], F32)
        junk = sb("d_junk", [P, 2 * D], F32)
        z = sb("d_z", [P, 1], F32)
        ez = sb("d_ez", [P, 1], F32)
        beta = sb("d_beta", [P, 1], F32)
        diff = sb("d_diff", [P, D], F32)
        base = sb("d_base", [P, D], F32)
        y = sb("d_y", [P, D], F32)
        stats = sb("d_stats", [P, 6], F32)
        mv = sb("d_mv", [P, 2], F32)
        lnv = sb("d_lnv", [P, 1], F32)
        rstd = sb("d_rstd", [P, 1], F32)
        y_out = sb("d_yout", [P, D], F32)

        ps_s = [ps(f"d_ps_s{i}", [P, SW], F32) for i in range(2)]
        ps_w = [ps(f"d_ps_w{i}", [P, TW], F32) for i in range(2)]
        ps_q = ps("d_ps_q", [P, P], F32)
        ps_o = ps("d_ps_o", [P, D], F32)

        tables_in = sem("tables_in")
        adj_loaded = sem("adj_loaded")
        rows_loaded = sem("rows_loaded")
        pen_ready = sem("pen_ready")
        q_turned = sem("q_turned")
        qT_ready = sem("qT_ready")
        scored = sem("scored")
        masked = sem("masked")
        shift_ready = sem("shift_ready")
        expd = sem("expd")
        turned = sem("turned")
        wT_ready = sem("wT_ready")
        summed = sem("summed")
        z_ready = sem("z_ready")
        ez_ready = sem("ez_ready")
        var_ready = sem("var_ready")
        rstd_ready = sem("rstd_ready")
        y_ready = sem("y_ready")
        y_stored = sem("y_stored")
        turn = sem("turn")

        def count(eng):
            return eng.value_load(n_dense[0:1, 0:1], min_val=1, max_val=T)

        def held(eng, sem, value):
            eng.wait_ge(sem, value)
            eng.sem_inc(turn, 1)

        block = ctx.enter_context(nc.Block())

        @block.sync
        def _(sp):
            sp.dma_start(kT[:], kt_dram).then_inc(tables_in, 16)
            sp.dma_start(v_rows[:], kv_dram[:, D:2 * D].rearrange("(b p) c -> p b c", p=P)).then_inc(tables_in, 16)
            n = count(sp)
            with sp.Fori(0, n) as i:
                tile = sp.value_load(tile_list[0:1, bass.ds(i, 1)], min_val=0, max_val=T - 1)
                row = sp.snap(tile * P)
                sp.wait_ge(pen_ready, i)
                sp.dma_start(adj_in[:], adj[bass.ds(row, P), :]).then_inc(adj_loaded, 16)
                sp.wait_ge(y_ready, i)
                sp.dma_start(q_in[:], qr_dram[bass.ds(row, P), 0:D]).then_inc(rows_loaded, 16)
                sp.dma_start(o_r[:, D:2 * D], qr_dram[bass.ds(row, P), D:2 * D]).then_inc(rows_loaded, 16)
                sp.dma_start(x_in[:], x[bass.ds(row, P), :]).then_inc(rows_loaded, 16)
                sp.wait_ge(y_ready, i + 1)
                sp.dma_start(out[bass.ds(row, P), :], y_out[:]).then_inc(y_stored, 16)
                sp.wait_ge(y_stored, 16 * i + 16)
                sp.sem_inc(turn, 1)

        @block.tensor
        def _(pe):
            pe.wait_ge(tables_in, 32)
            n = count(pe)
            with pe.Fori(0, n) as i:
                pe.wait_ge(rows_loaded, 48 * i + 48)
                nc.tensor.transpose(ps_q[:], q_in[:], ident[:]).then_inc(q_turned, 1)
                pe.wait_ge(qT_ready, i + 1)

                def scores(h):
                    for g in range(SG):
                        pe.wait_ge(masked, H * SG * i + (h * SG + g - 1)) if h * SG + g >= 2 else None
                        for k in range(SW // 512):
                            col = g * SW + k * 512
                            last = nc.tensor.matmul(ps_s[g % 2][:, k * 512:(k + 1) * 512], qT[h * C:(h + 1) * C, :],
                                                    kT[h * C:(h + 1) * C, col:col + 512], start=True, stop=True)
                        last.then_inc(scored, 1)

                scores(0)
                for h in range(H):
                    if h + 1 < H:
                        scores(h + 1)
                    for g in range(TG):
                        step = TG * (H * i + h) + g
                        pe.wait_ge(expd, (N // EW) * (H * i + h) + g * TW // EW + 1)
                        for k in range(TW // P):
                            col = g * TW + k * P
                            last = nc.tensor.transpose(ps_w[g % 2][:, k * P:(k + 1) * P], sc[:, h % 2, col:col + P],
                                                       ident[:])
                        last.then_inc(turned, 1)
                        pe.wait_ge(wT_ready, step + 1)
                        for k in range(TW // P):
                            b = g * (TW // P) + k
                            last = nc.tensor.matmul(ps_o[:, h * C:(h + 1) * C], wT[:, g % 2, k * P:(k + 1) * P],
                                                    v_rows[:, b, h * C:(h + 1) * C], start=(b == 0), stop=(b == T - 1))
                        last.then_inc(summed, 1)
                pe.wait_ge(z_ready, i + 1)
                pe.sem_inc(turn, 1)

        @block.scalar
        def _(act):
            act.preload_act_table_set("natural_log_exp_and_others")
            n = count(act)
            with act.Fori(0, n) as i:
                act.wait_ge(q_turned, i + 1)
                nc.scalar.copy(qT[:], ps_q[:]).then_inc(qT_ready, 1)
                for h in range(H):
                    act.wait_ge(shift_ready, H * i + h + 1)
                    for k in range(N // EW):
                        part = sc[:, h % 2, k * EW:(k + 1) * EW]
                        nc.scalar.activation(part, part, ACT.Exp, bias=shift[:, h:h + 1], scale=SCALE,
                                             accum_out=dsum[:, h, k:k + 1]).then_inc(expd, 1)
                    for g in range(TG):
                        step = TG * (H * i + h) + g
                        act.wait_ge(turned, step + 1)
                        nc.scalar.copy(wT[:, g % 2], ps_w[g % 2][:]).then_inc(wT_ready, 1)
                act.wait_ge(z_ready, i + 1)
                nc.scalar.activation(ez[:], z[:], ACT.Exp, scale=-1.0).then_inc(ez_ready, 1)
                act.wait_ge(var_ready, i + 1)
                nc.scalar.activation(lnv[:], mv[:, 1:2], ACT.Ln, bias=eps_col[:])
                act.drain()
                nc.scalar.activation(rstd[:], lnv[:], ACT.Exp, scale=-0.5).then_inc(rstd_ready, 1)

        @block.vector
        def _(dve):
            n = count(dve)
            with dve.Fori(0, n) as i:
                dve.wait_ge(adj_loaded, 16 * i + 16)
                nc.vector.tensor_scalar(pen[:], adj_in[:], 0.0, MASKED, ALU.is_equal, ALU.mult).then_inc(pen_ready, 1)
                dve.drain()
                for h in range(H):
                    for g in range(SG):
                        held(dve, scored, H * SG * i + h * SG + g + 1)
                        if g == 0 and h >= 2:
                            held(dve, turned, TG * (H * i + h - 1))
                        nc.vector.tensor_tensor_reduce(
                            out=sc[:, h % 2, g * SW:(g + 1) * SW], in0=ps_s[g % 2][:], in1=pen[:, g * SW:(g + 1) * SW],
                            scale=1.0, scalar=FLOOR, op0=ALU.add, op1=ALU.max,
                            accum_out=gmax[:, h, g:g + 1]).then_inc(masked, 1)
                    dve.drain()
                    nc.vector.tensor_reduce(z[:], gmax[:, h], AX, ALU.max)
                    dve.drain()
                    nc.vector.tensor_scalar(shift[:, h:h + 1], z[:], -SCALE, None, ALU.mult).then_inc(shift_ready, 1)
                dve.wait_ge(expd, (N // EW) * H * (i + 1))
                nc.vector.tensor_reduce(den[:], dsum[:], AX, ALU.add)
                dve.drain()
                nc.vector.tensor_scalar(isz[:], den[:], 0.0, None, ALU.is_equal)
                dve.drain()
                nc.vector.tensor_tensor(den[:], den[:], isz[:], ALU.add)
                dve.drain()
                nc.vector.reciprocal(rden[:], den[:])
                dve.drain()
                dve.wait_ge(summed, TG * H * (i + 1))
                dve.wait_ge(rows_loaded, 48 * i + 48)
                nc.vector.tensor_tensor(o_r[:, 0:D].rearrange("p (c h) -> p h c", h=H),
                                        ps_o[:].rearrange("p (h c) -> p h c", h=H),
                                        rden[:].unsqueeze(2).to_broadcast([P, H, C]), ALU.mult)
                dve.drain()
                nc.vector.tensor_tensor_reduce(out=junk[:], in0=o_r[:], in1=gate_w[:], scale=1.0, scalar=0.0,
                                               op0=ALU.mult, op1=ALU.add, accum_out=z[:]).then_inc(z_ready, 1)
                nc.vector.tensor_tensor(diff[:], o_r[:, D:2 * D], o_r[:, 0:D], ALU.subtract)
                nc.vector.tensor_tensor(base[:], x_in[:], o_r[:, 0:D], ALU.add)
                dve.wait_ge(ez_ready, i + 1)
                nc.vector.tensor_scalar(ez[:], ez[:], 1.0, None, ALU.add)
                dve.drain()
                nc.vector.reciprocal(beta[:], ez[:])
                dve.drain()
                nc.vector.scalar_tensor_tensor(out=y[:], in0=diff[:], scalar=beta[:], in1=base[:], op0=ALU.mult,
                                               op1=ALU.add)
                dve.drain()
                nc.vector.bn_stats(stats[:], y[:])
                dve.drain()
                nc.vector.bn_aggr(mv[:], stats[:]).then_inc(var_ready, 1)
                dve.wait_ge(rstd_ready, i + 1)
                dve.wait_ge(y_stored, 16 * i)
                nc.vector.tensor_scalar(y_out[:], y[:], mv[:, 0:1], rstd[:], ALU.subtract, ALU.mult).then_inc(y_ready, 1)


_INS = ['x', 'adj', 'L0_gnn_Wq', 'L0_gnn_bq', 'L0_gnn_Wk', 'L0_gnn_bk', 'L0_gnn_Wv', 'L0_gnn_bv', 'L0_gnn_Ws',
        'L0_gnn_bs', 'L0_gnn_Wb']


def kernel(**inputs):
    import numpy as _np
    import concourse.bacc as _bacc
    from concourse import mybir as _mybir
    from concourse.bass_utils import run_bass_kernel_spmd as _run

    nc = _bacc.Bacc("TRN2", target_bir_lowering=False, num_devices=1)
    arrays, args = {}, []
    for name in _INS:
        a = _np.ascontiguousarray(inputs[name])
        arrays[f"in_{name}"] = a
        args.append(nc.dram_tensor(f"in_{name}", a.shape, _mybir.dt.from_np(a.dtype), kind="ExternalInput").ap())
    args.append(nc.dram_tensor("out_rows", (8192, 128), _mybir.dt.float32, kind="ExternalOutput").ap())
    gnn_resnorm_kernel(nc, *args)
    r = _run(nc, [arrays], core_ids=[0])
    return r.results[0]["out_rows"]
```

```python
import concourse.bass as bass
from concourse import mybir
from contextlib import ExitStack

F32 = mybir.dt.float32
BF16 = mybir.dt.bfloat16
U16 = mybir.dt.uint16
U32 = mybir.dt.uint32
I32 = mybir.dt.int32
ALU = mybir.AluOpType
ACT = mybir.ActivationFunctionType
AX = mybir.AxisListType.X

P = 128
N = 8192
D = 128
H, C = 4, 32
T = N // P
SCALE = float(C) ** -0.5
EPS = 1e-5
MASKED = -1e30
FLOOR = -1e29
GROUP = 4


def gnn_resnorm_kernel(nc, x, adj, Wq, bq, Wk, bk, Wv, bv, Ws, bs, Wb, out):
    outer = ExitStack()
    with outer:
        kv_dram = nc.dram_tensor("kv_rows", (N, 2 * D), F32, kind="Internal").ap()
        qr_dram = nc.dram_tensor("qr_rows", (N, 2 * D), F32, kind="Internal").ap()
        kt_dram = nc.dram_tensor("k_columns", (D, N), F32, kind="Internal").ap()

        def keep(name, shape, dt):
            return outer.enter_context(nc.sbuf_tensor(name, shape, dt))

        ident = keep("ident", [P, P], F32)
        gate_w = keep("gate_w", [P, 2 * D], F32)
        eps_col = keep("eps_col", [P, 1], F32)
        tile_list = keep("tile_list", [1, T], I32)
        n_dense = keep("n_dense", [1, 1], I32)

        project_nodes(nc, x, Wq, bq, Wk, bk, Wv, bv, Ws, bs, Wb, kv_dram, qr_dram, kt_dram,
                      ident, gate_w, eps_col)
        sparse_tiles(nc, x, adj, kv_dram, qr_dram, ident, gate_w, eps_col, tile_list, n_dense, out)
        dense_tiles(nc, x, adj, kv_dram, qr_dram, kt_dram, ident, gate_w, eps_col, tile_list, n_dense, out)


def project_nodes(nc, x, Wq, bq, Wk, bk, Wv, bv, Ws, bs, Wb, kv_dram, qr_dram, kt_dram,
                  ident, gate_w, eps_col):
    ctx = ExitStack()
    with ctx:
        def sb(name, shape, dt):
            return ctx.enter_context(nc.sbuf_tensor(name, shape, dt))

        def ps(name, shape, dt):
            return ctx.enter_context(nc.psum_tensor(name, shape, dt))

        def sem(name):
            return ctx.enter_context(nc.semaphore(name))

        w_all = sb("w_all", [P, 4 * D], F32)
        b_row = sb("b_row", [1, 4 * D], F32)
        b_all = sb("b_all", [P, 4 * D], F32)
        bk_col = sb("bk_col", [P, 1], F32)
        wb_row = sb("wb_row", [1, 3 * D], F32)
        gw_row = sb("gw_row", [1, 2 * D], F32)
        ones = sb("ones", [1, P], F32)
        x_in = sb("x_in", [P, 2, GROUP, D], F32)
        xT = sb("xT", [P, 2, GROUP * P], F32)
        rows = sb("rows", [P, 2, GROUP, 4 * D], F32)
        kT = sb("kT", [P, 2, GROUP * P], F32)
        ps_t = [ps(f"ps_t{i}", [P, GROUP * P], F32) for i in range(2)]
        ps_r = [ps(f"ps_r{i}", [P, 4 * D], F32) for i in range(4)]
        ps_k = [ps(f"ps_k{i}", [P, GROUP * P], F32) for i in range(2)]

        weights_in = sem("weights_in")
        x_loaded = [sem(f"x_loaded{i}") for i in range(2)]
        const_ready = sem("const_ready")
        bias_spread = sem("bias_spread")
        bias_ready = sem("bias_ready")
        x_turned = sem("x_turned")
        xT_ready = sem("xT_ready")
        rows_summed = sem("rows_summed")
        rows_ready = sem("rows_ready")
        kT_summed = sem("kT_summed")
        kT_ready = sem("kT_ready")
        stored = [sem(f"stored{i}") for i in range(2)]
        sp_turn = sem("sp_turn")

        def node_rows(a, row):
            return a[bass.ds(row, GROUP * P), :].rearrange("(j p) c -> p j c", p=P)

        block = ctx.enter_context(nc.Block())

        @block.sync
        def _(sp):
            for k, w in enumerate((Wk, Wv, Wq, Ws)):
                sp.dma_start(w_all[:, k * D:(k + 1) * D], w).then_inc(weights_in, 16)
            for k, b in enumerate((bk, bv, bq, bs)):
                sp.dma_start(b_row[0:1, k * D:(k + 1) * D], b.rearrange("(a c) -> a c", a=1)).then_inc(weights_in, 16)
            sp.dma_start(bk_col[:], bk.rearrange("(c a) -> c a", a=1)).then_inc(weights_in, 16)
            sp.dma_start(wb_row[:], Wb.rearrange("c a -> a c")).then_inc(weights_in, 16)
            for g in range(2):
                sp.dma_start(x_in[:, g], node_rows(x, g * GROUP * P)).then_inc(x_loaded[g], 16)
            with sp.Fori(0, T // GROUP // 2) as i:
                for g in range(2):
                    row = sp.snap((2 * i + g) * (GROUP * P))
                    ahead = sp.snap(((2 * i + g + 2) % (T // GROUP)) * (GROUP * P))
                    sp.wait_ge(rows_ready, GROUP * (2 * i + g + 2))
                    sp.dma_start(node_rows(kv_dram, row), rows[:, g, :, 0:2 * D]).then_inc(stored[g], 16)
                    sp.dma_start(node_rows(qr_dram, row), rows[:, g, :, 2 * D:4 * D]).then_inc(stored[g], 16)
                    sp.wait_ge(kT_ready, 2 * i + g + 1)
                    sp.sem_inc(sp_turn, 1)
                    sp.dma_start(kt_dram[:, bass.ds(row, GROUP * P)], kT[:, g]).then_inc(stored[g], 16)
                    sp.dma_start(x_in[:, g], node_rows(x, ahead)).then_inc(x_loaded[g], 16)
            for g in range(2):
                sp.wait_ge(stored[g], 48 * (T // GROUP // 2))
                sp.wait_ge(x_loaded[g], 16 * (T // GROUP // 2 + 1))

        @block.gpsimd
        def _(pool):
            nc.gpsimd.memset(ones[:], 1.0).then_inc(const_ready, 1)
            nc.gpsimd.memset(eps_col[:], EPS).then_inc(const_ready, 1)
            nc.gpsimd.memset(ident[:], 0.0).then_inc(const_ready, 1)
            pool.wait_ge(const_ready, 3)
            nc.gpsimd.affine_select(out=ident[:], in_=ident[:], compare_op=ALU.not_equal, fill=1.0, base=0,
                                    pattern=[[-1, P]], channel_multiplier=1).then_inc(const_ready, 1)

        @block.tensor
        def _(pe):
            pe.wait_ge(weights_in, 160)
            pe.wait_ge(const_ready, 4)
            pe.wait_ge(bias_spread, 1)
            nc.tensor.matmul(ps_r[0][:], ones[:], b_row[:], start=True, stop=True)
            nc.tensor.matmul(ps_r[1][:, 0:2 * D], ones[:], gw_row[:], start=True, stop=True).then_inc(rows_summed, 1)
            pe.wait_ge(bias_ready, 1)
            with pe.Fori(0, T // GROUP // 2) as i:
                for g in range(2):
                    grp = 2 * i + g
                    pe.wait_ge(x_loaded[g], 16 * i + 16)
                    for j in range(GROUP):
                        last = nc.tensor.transpose(ps_t[g][:, j * P:(j + 1) * P], x_in[:, g, j], ident[:])
                    last.then_inc(x_turned, 1)
                    pe.wait_ge(xT_ready, grp + 1)
                    nc.tensor.matmul(ps_k[g][:], w_all[:, 0:D], xT[:, g], start=True, stop=True).then_inc(kT_summed, 1)
                    for j in range(GROUP):
                        pe.wait_ge(rows_ready, GROUP * grp + j + 1)
                        nc.tensor.matmul(ps_r[j][:], xT[:, g, j * P:(j + 1) * P], w_all[:], start=True,
                                         stop=True).then_inc(rows_summed, 1)

        @block.scalar
        def _(act):
            act.wait_ge(weights_in, 160)
            with act.Fori(0, T // GROUP // 2) as i:
                for g in range(2):
                    grp = 2 * i + g
                    act.wait_ge(x_turned, grp + 1)
                    nc.scalar.copy(xT[:, g], ps_t[g][:]).then_inc(xT_ready, 1)
                    act.wait_ge(stored[g], 48 * i)
                    act.wait_ge(kT_summed, grp + 1)
                    nc.scalar.activation(kT[:, g], ps_k[g][:], ACT.Identity, bias=bk_col[:]).then_inc(kT_ready, 1)

        @block.vector
        def _(dve):
            dve.wait_ge(weights_in, 160)
            nc.vector.tensor_tensor(gw_row[0:1, 0:D], wb_row[0:1, 0:D], wb_row[0:1, 2 * D:3 * D], ALU.add)
            nc.vector.tensor_tensor(gw_row[0:1, D:2 * D], wb_row[0:1, D:2 * D], wb_row[0:1, 2 * D:3 * D],
                                    ALU.subtract).then_inc(bias_spread, 1)
            dve.wait_ge(rows_summed, 1)
            nc.vector.tensor_copy(b_all[:], ps_r[0][:])
            nc.vector.tensor_copy(gate_w[:], ps_r[1][:, 0:2 * D]).then_inc(bias_ready, 1)
            dve.drain()
            dve.sem_inc(rows_ready, GROUP)
            with dve.Fori(0, T // GROUP // 2) as i:
                for g in range(2):
                    dve.wait_ge(stored[g], 48 * i)
                    for j in range(GROUP):
                        dve.wait_ge(rows_summed, 4 * (2 * i + g) + j + 2)
                        nc.vector.tensor_tensor(rows[:, g, j], ps_r[j][:], b_all[:], ALU.add).then_inc(rows_ready, 1)


def sparse_tiles(nc, x, adj, kv_dram, qr_dram, ident, gate_w, eps_col, tile_list, n_dense, out):
    HALF = N // 2
    RING = 3
    MAX_S = 24
    NO_EDGE = N

    SHAPES = [(1, 4, 20, 32, 16), (2, 4, 16, 32, 16), (3, 4, 15, 32, 16), (4, 3, 17, 32, 16), (5, 2, 22, 16, 8),
              (11, 2, 17, 16, 8), (20, 1, 24, 16, 8), (29, 1, 22, 16, 8)]

    def valid(t):
        return 1 <= t < T

    def shape(t):
        return [s for s in SHAPES if s[0] <= t][-1][1:] if valid(t) else None

    def n_chunks(t):
        return shape(t)[0] if valid(t) else 0

    def slots(t):
        return shape(t)[1]

    def cap(t):
        return n_chunks(t) * slots(t)

    def chunks_before(t):
        return sum(n_chunks(u) for u in range(1, t))

    def multi_upto(t):
        return sum(n_chunks(u) > 1 for u in range(1, t + 1))

    def slots_landed(t, c):
        g = chunks_before(t) + c
        at, total = 0, 0
        for u in range(1, t + 1):
            for _ in range(n_chunks(u)):
                if at <= g and at % RING == g % RING:
                    total += 16 * slots(u)
                at += 1
        return total

    def runs(sign):
        t, found = -2, []
        while t <= T:
            e = t
            while e <= T and sign(e) == sign(t):
                e += 1
            bodies = (e - t) // RING
            if bodies >= 2:
                found.append((t, bodies))
                t += RING * bodies
            else:
                found.append((t, None))
                t += 1
        return found

    def program(eng, sign, step):
        for t0, bodies in runs(sign):
            if bodies is None:
                step(t0, t0, None)
            else:
                with eng.Fori(0, bodies) as i:
                    for u in range(RING):
                        step(t0 + u, eng.snap(i * RING + (t0 + u)), i)

    def lin(count, t, i):
        return count(t) if i is None else count(t) + i * (count(t + RING) - count(t))

    ctx = ExitStack()
    with ctx:
        def sb(name, shape, dt):
            return ctx.enter_context(nc.sbuf_tensor("s_" + name, shape, dt))

        def sem(name):
            return ctx.enter_context(nc.semaphore("s_" + name))

        adj_in = sb("adj", [P, RING, HALF], F32)
        mask = sb("mask", [P, RING, HALF], BF16)
        keys = sb("keys", [P, N], U16)
        kv = sb("kv", [P, RING, MAX_S, 2 * D], F32)
        prod = sb("prod", [P, MAX_S, D], F32)
        cand = sb("cand", [P, 8 * 48], F32)
        top = sb("top", [P, 80], F32)
        empty = sb("empty", [P, RING, 80], F32)
        idx = sb("idx", [P, RING, 80], U32)
        q_in = sb("q", [P, RING, D], F32)
        o_r = sb("or", [P, RING, 2 * D], F32)
        x_in = sb("x", [P, RING, D], F32)
        raw = sb("raw", [P, MAX_S * H], F32)
        sc = sb("sc", [P, MAX_S * H], F32)
        e = sb("e", [P, MAX_S * H], F32)
        peak = sb("peak", [P, RING, 4, H], F32)
        dens = sb("dens", [P, RING, 4, H], F32)
        below = sb("below", [P, RING, 4, H], F32)
        share = sb("share", [P, RING, 4, H], F32)
        mtop = sb("mtop", [P, H], F32)
        parts = sb("parts", [P, 4, D], F32)
        osum = sb("osum", [P, D], F32)
        dtmp = sb("dtmp", [P, 4, H], F32)
        den = sb("den", [P, H], F32)
        isz = sb("isz", [P, H], F32)
        rden = sb("rden", [P, H], F32)
        junk = sb("junk", [P, 2 * D], F32)
        z = sb("z", [P, RING], F32)
        ez = sb("ez", [P, RING], F32)
        beta = sb("beta", [P, 1], F32)
        diff = sb("diff", [P, D], F32)
        base = sb("base", [P, D], F32)
        y = sb("y", [P, D], F32)
        stats = sb("stats", [P, 6], F32)
        mv = sb("mv", [P, RING, 2], F32)
        lnv = sb("lnv", [P, 1], F32)
        rstd = sb("rstd", [P, RING], F32)
        y_out = sb("yout", [P, RING, D], F32)
        edges = sb("edges", [P, T, 2], F32)
        unused = sb("unused", [P, T], F32)
        caps = sb("caps", [P, T], F32)
        over = sb("over", [P, T], F32)
        ones = sb("ones", [P, 1], F32)
        order = sb("order", [1, T], F32)
        left = sb("left", [1, T], F32)
        ranked = sb("ranked", [1, T], F32)
        nleft = sb("nleft", [1, 1], F32)

        acc = [ctx.enter_context(nc.psum_tensor(f"s_acc{i}", [P, 4, D], F32)) for i in range(RING)]
        ps_f = ctx.enter_context(nc.psum_tensor("s_ps_f", [1, T], F32))

        consts = sem("consts")
        adj_loaded = [sem(f"adj_loaded{i}") for i in range(RING)]
        adj_used = sem("adj_used")
        masked = sem("masked")
        scanned = sem("scanned")
        idx_ready = sem("idx_ready")
        gathered = [sem(f"gathered{i}") for i in range(RING)]
        rows_loaded = [sem(f"rows_loaded{i}") for i in range(RING)]
        shifted = sem("shifted")
        expd = sem("expd")
        weighted = sem("weighted")
        summed = sem("summed")
        below_ready = sem("below_ready")
        share_ready = sem("share_ready")
        z_ready = sem("z_ready")
        ez_ready = sem("ez_ready")
        var_ready = sem("var_ready")
        rstd_ready = sem("rstd_ready")
        y_ready = sem("y_ready")
        y_stored = [sem(f"y_stored{i}") for i in range(RING)]
        over_ready = sem("over_ready")
        over_summed = sem("over_summed")
        turn = sem("turn")

        def need(eng, sem, value, carry=False):
            if isinstance(value, int) and value <= 0:
                return
            eng.wait_ge(sem, value)
            if carry:
                eng.sem_inc(turn, 1)

        def half_no(t, i, h):
            return lin(lambda u: 2 * (u - 1) + h + 1, t, i)

        def chunk_no(t, i, c):
            return lin(lambda u: chunks_before(u) + c + 1, t, i)

        def ring_no(t, i):
            return lin(lambda u: (u - 1) // RING + 1, t, i)

        def adj_no(t, i, h):
            return lin(lambda u: (2 * (u - 1) + h) // RING + 1, t, i)

        def half_slot(t, h):
            return (2 * (t - 1) + h) % RING

        def kv_slot(t, c):
            return (chunks_before(t) + c) % RING

        CONSTS = 7 + len(SHAPES)
        block = ctx.enter_context(nc.Block())

        @block.sync
        def _(sp):
            def step(t, tt, i):
                for h in range(2):
                    if valid(t + 4):
                        row = sp.snap((tt + 4) * P) if i is not None else (t + 4) * P
                        need(sp, adj_used, half_no(t + 4, i, h) - RING, i is not None)
                        sp.dma_start(adj_in[:, half_slot(t + 4, h)],
                                     adj[bass.ds(row, P), h * HALF:(h + 1) * HALF]
                                     ).then_inc(adj_loaded[half_slot(t + 4, h)], 16)
                if valid(t - 1):
                    row = sp.snap((tt - 1) * P) if i is not None else (t - 1) * P
                    need(sp, y_ready, lin(lambda u: u - 1, t, i), i is not None)
                    sp.dma_start(out[bass.ds(row, P), :], y_out[:, (t - 1) % RING]).then_inc(y_stored[(t - 1) % RING], 16)
                if valid(t + 2):
                    r = (t + 2) % RING
                    row = sp.snap((tt + 2) * P) if i is not None else (t + 2) * P
                    sp.dma_start(q_in[:, r], qr_dram[bass.ds(row, P), 0:D]).then_inc(rows_loaded[r], 16)
                    sp.dma_start(o_r[:, r, D:2 * D], qr_dram[bass.ds(row, P), D:2 * D]).then_inc(rows_loaded[r], 16)
                    sp.dma_start(x_in[:, r], x[bass.ds(row, P), :]).then_inc(rows_loaded[r], 16)

            for h in range(2):
                sp.dma_start(adj_in[:, half_slot(1, h)], adj[P:2 * P, h * HALF:(h + 1) * HALF]
                             ).then_inc(adj_loaded[half_slot(1, h)], 16)
            program(sp, lambda t: (valid(t + 4), valid(t - 1), valid(t + 2)), step)
            for r in range(RING):
                sp.wait_ge(y_stored[r], 16 * sum(t % RING == r for t in range(1, T)))

        @block.gpsimd
        def _(pool):
            nc.gpsimd.iota(keys[:], pattern=[[-1, N]], base=N, channel_multiplier=0).then_inc(consts, 1)
            nc.gpsimd.iota(order[:], pattern=[[-1, T]], base=T, channel_multiplier=0,
                           allow_small_or_imprecise_dtypes=True).then_inc(consts, 1)
            nc.gpsimd.memset(kv[:], 0.0).then_inc(consts, 1)
            nc.gpsimd.memset(edges[:, 0], 0.0).then_inc(consts, 1)
            nc.gpsimd.memset(unused[:, 0:1], 0.0).then_inc(consts, 1)
            nc.gpsimd.memset(caps[:, 0:1], -1.0).then_inc(consts, 1)
            for k, s in enumerate(SHAPES):
                end = SHAPES[k + 1][0] if k + 1 < len(SHAPES) else T
                nc.gpsimd.memset(caps[:, s[0]:end], float(s[1] * s[2])).then_inc(consts, 1)
            nc.gpsimd.memset(ones[:], 1.0).then_inc(consts, 1)
            pool.wait_ge(consts, CONSTS)
            last_node = pool.to_reg(N - 1)

            def step(t, tt, i):
                if not valid(t):
                    return
                need(pool, idx_ready, lin(lambda u: u, t, i), True)
                for c in range(n_chunks(t)):
                    need(pool, summed, lin(lambda u: chunks_before(u) + c + 1 - RING, t, i), True)
                    for s in range(slots(t)):
                        col = c * slots(t) + s
                        nc.gpsimd.indirect_dma_start(
                            out=kv[:, kv_slot(t, c), s], out_offset=None, in_=kv_dram[:, :],
                            in_offset=bass.IndirectOffsetOnAxis(ap=idx[:, t % RING, col:col + 1], axis=0),
                            bounds_check=last_node, oob_is_err=False).then_inc(gathered[kv_slot(t, c)], 16)

            program(pool, lambda t: shape(t), step)

        @block.tensor
        def _(pe):
            def step(t, tt, i):
                if not valid(t):
                    return
                for c in range(n_chunks(t)):
                    need(pe, weighted, chunk_no(t, i, c))
                    for s in range(slots(t)):
                        last = nc.tensor.matmul(acc[t % RING][:, c], ident[:], kv[:, kv_slot(t, c), s, D:2 * D],
                                                start=(s == 0), stop=(s == slots(t) - 1))
                    last.then_inc(summed, 1)

            program(pe, lambda t: shape(t), step)
            pe.wait_ge(over_ready, 1)
            nc.tensor.matmul(ps_f[:], ones[:], over[:], start=True, stop=True).then_inc(over_summed, 1)

        @block.scalar
        def _(act):
            act.preload_act_table_set("natural_log_exp_and_others")

            def exp_chunk(t, i, c):
                need(act, shifted, chunk_no(t, i, c))
                w = slots(t) * H
                nc.scalar.activation(e[:, 0:w], sc[:, 0:w], ACT.Exp, scale=SCALE).then_inc(expd, 1)

            def mask_half(t, tt, i, h):
                b = half_slot(t, h)
                need(act, adj_loaded[b], lin(lambda u: 16 * ((2 * (u - 1) + h) // RING + 1), t, i))
                need(act, scanned, half_no(t, i, h) - RING)
                nc.scalar.activation(mask[:, b], adj_in[:, b], ACT.Sign).then_inc(adj_used, 1)
                act.drain()
                nc.scalar.activation(mask[:, b], mask[:, b], ACT.Square,
                                     accum_out=edges[:, bass.ds(tt, 1), h]).then_inc(masked, 1)

            def step(t, tt, i):
                if valid(t):
                    exp_chunk(t, i, 0)
                if valid(t - 1):
                    r = (t - 1) % RING
                    need(act, z_ready, lin(lambda u: u - 1, t, i))
                    nc.scalar.activation(ez[:, r:r + 1], z[:, r:r + 1], ACT.Exp, scale=-1.0).then_inc(ez_ready, 1)
                ahead = None
                if valid(t + 3):
                    ahead = act.snap(tt + 3) if i is not None else t + 3
                    mask_half(t + 3, ahead, i, 0)
                if valid(t - 1):
                    r = (t - 1) % RING
                    need(act, var_ready, lin(lambda u: u - 1, t, i))
                    nc.scalar.activation(lnv[:], mv[:, r, 1:2], ACT.Ln, bias=eps_col[:])
                    act.drain()
                    nc.scalar.activation(rstd[:, r:r + 1], lnv[:], ACT.Exp, scale=-0.5).then_inc(rstd_ready, 1)
                if valid(t + 3):
                    mask_half(t + 3, ahead, i, 1)
                if valid(t):
                    for c in range(1, n_chunks(t)):
                        exp_chunk(t, i, c)
                    if n_chunks(t) > 1:
                        r = t % RING
                        need(act, below_ready, lin(multi_upto, t, i))
                        nc.scalar.activation(share[:, r, 0:n_chunks(t)], below[:, r, 0:n_chunks(t)], ACT.Exp,
                                             scale=SCALE).then_inc(share_ready, 1)

            program(act, lambda t: (shape(t), n_chunks(t - 1), valid(t + 3), valid(t - 1)), step)

        @block.vector
        def _(dve):
            def score_chunk(t, i, c):
                r, b, s = t % RING, kv_slot(t, c), slots(t)
                if c == 0:
                    need(dve, rows_loaded[r], lin(lambda u: 48 * ((u - 1) // RING + 1), t, i))
                need(dve, gathered[b], lin(lambda u: slots_landed(u, c), t, i))
                nc.vector.tensor_tensor(prod[:, 0:s], kv[:, b, 0:s, 0:D],
                                        q_in[:, r].unsqueeze(1).to_broadcast([P, s, D]), ALU.mult)
                dve.drain()
                nc.vector.tensor_reduce(raw[:, 0:s * H], prod[:, 0:s].rearrange("p s (h c) -> p (s h) c", h=H), AX,
                                        ALU.add)
                dve.drain()
                sc_sh = sc[:, 0:s * H].rearrange("p (s h) -> p s h", h=H)
                nc.vector.scalar_tensor_tensor(
                    out=sc_sh, in0=empty[:, r, c * s:(c + 1) * s].unsqueeze(2).to_broadcast([P, s, H]), scalar=MASKED,
                    in1=raw[:, 0:s * H].rearrange("p (s h) -> p s h", h=H), op0=ALU.mult, op1=ALU.add)
                dve.drain()
                nc.vector.tensor_reduce(mtop[:], sc[:, 0:s * H].rearrange("p (s h) -> p h s", h=H), AX, ALU.max)
                dve.drain()
                nc.vector.tensor_scalar(peak[:, r, c], mtop[:], FLOOR, None, ALU.max)
                dve.drain()
                nc.vector.tensor_tensor(sc_sh, sc_sh, peak[:, r, c].unsqueeze(1).to_broadcast([P, s, H]),
                                        ALU.subtract).then_inc(shifted, 1)

            def weigh_chunk(t, i, c):
                r, b, s = t % RING, kv_slot(t, c), slots(t)
                need(dve, expd, chunk_no(t, i, c))
                v = kv[:, b, 0:s, D:2 * D].rearrange("p s (h c) -> p s h c", h=H)
                e_sh = e[:, 0:s * H].rearrange("p (s h) -> p s h", h=H)
                nc.vector.tensor_tensor(v, v, e_sh.unsqueeze(3).to_broadcast([P, s, H, C]), ALU.mult).then_inc(weighted, 1)
                nc.vector.tensor_reduce(dens[:, r, c], e[:, 0:s * H].rearrange("p (s h) -> p h s", h=H), AX, ALU.add)

            def scan_half(t, i, h):
                b = half_slot(t, h)
                n_seg = shape(t)[2 + h]
                first = shape(t)[2] * h
                need(dve, masked, half_no(t, i, h))
                key = mask[:, b].bitcast(U16)
                nc.vector.tensor_tensor(key, mask[:, b], keys[:, h * HALF:(h + 1) * HALF], ALU.mult)
                dve.drain()
                seg = key.rearrange("p (j s) -> p s j", s=n_seg)
                for s in range(n_seg):
                    last = nc.vector.max(cand[:, 8 * (first + s):8 * (first + s + 1)], seg[:, s])
                last.then_inc(scanned, 1)

            def list_edges(t, tt, i):
                r = t % RING
                width = 8 * (shape(t)[2] + shape(t)[3])
                rounds = -(-cap(t) // 8)
                dve.drain()
                for k in range(rounds):
                    nc.vector.max(top[:, 8 * k:8 * k + 8], cand[:, 0:width])
                    dve.drain()
                    if k + 1 < rounds:
                        nc.vector.match_replace(cand[:, 0:width], top[:, 8 * k:8 * k + 8], cand[:, 0:width], 0.0)
                        dve.drain()
                nc.vector.tensor_scalar(idx[:, r, 0:cap(t)], top[:, 0:cap(t)], -1.0, float(NO_EDGE), ALU.mult,
                                        ALU.add).then_inc(idx_ready, 1)
                nc.vector.tensor_scalar(empty[:, r, 0:cap(t)], top[:, 0:cap(t)], 0.0, None, ALU.is_equal)
                dve.drain()
                nc.vector.tensor_reduce(unused[:, bass.ds(tt, 1)], empty[:, r, 0:cap(t)], AX, ALU.add)

            def join_chunks(t, i):
                r, n = t % RING, n_chunks(t)
                nc.vector.tensor_reduce(mtop[:], peak[:, r, 0:n].rearrange("p n h -> p h n"), AX, ALU.max)
                dve.drain()
                nc.vector.tensor_tensor(below[:, r, 0:n], peak[:, r, 0:n], mtop[:].unsqueeze(1).to_broadcast([P, n, H]),
                                        ALU.subtract).then_inc(below_ready, 1)

            def attend(t, i):
                r, n = t % RING, n_chunks(t)
                sums, total = acc[r][:, 0], dens[:, r, 0]
                dve.drain()
                need(dve, summed, lin(lambda u: chunks_before(u + 1), t, i))
                if n > 1:
                    need(dve, share_ready, lin(multi_upto, t, i))
                    w = share[:, r, 0:n]
                    nc.vector.tensor_tensor(parts[:, 0:n].rearrange("p n (h c) -> p (n h) c", h=H),
                                            acc[r][:, 0:n].rearrange("p n (h c) -> p (n h) c", h=H),
                                            w.rearrange("p n h -> p (n h)").unsqueeze(2).to_broadcast([P, n * H, C]),
                                            ALU.mult)
                    nc.vector.tensor_tensor(dtmp[:, 0:n], dens[:, r, 0:n], w, ALU.mult)
                    dve.drain()
                    nc.vector.tensor_reduce(osum[:], parts[:, 0:n].rearrange("p n c -> p c n"), AX, ALU.add)
                    nc.vector.tensor_reduce(den[:], dtmp[:, 0:n].rearrange("p n h -> p h n"), AX, ALU.add)
                    dve.drain()
                    sums, total = osum[:], den[:]
                nc.vector.tensor_scalar(isz[:], total, 0.0, None, ALU.is_equal)
                dve.drain()
                nc.vector.tensor_tensor(isz[:], total, isz[:], ALU.add)
                dve.drain()
                nc.vector.reciprocal(rden[:], isz[:])
                dve.drain()
                nc.vector.tensor_tensor(o_r[:, r, 0:D].rearrange("p (c h) -> p h c", h=H),
                                        sums.rearrange("p (h c) -> p h c", h=H),
                                        rden[:].unsqueeze(2).to_broadcast([P, H, C]), ALU.mult)
                dve.drain()
                nc.vector.tensor_tensor_reduce(out=junk[:], in0=o_r[:, r], in1=gate_w[:], scale=1.0, scalar=0.0,
                                               op0=ALU.mult, op1=ALU.add, accum_out=z[:, r:r + 1]).then_inc(z_ready, 1)
                nc.vector.tensor_tensor(diff[:], o_r[:, r, D:2 * D], o_r[:, r, 0:D], ALU.subtract)
                nc.vector.tensor_tensor(base[:], x_in[:, r], o_r[:, r, 0:D], ALU.add)

            def gate(t, i):
                r = t % RING
                need(dve, ez_ready, lin(lambda u: u, t, i))
                nc.vector.tensor_scalar(ez[:, r:r + 1], ez[:, r:r + 1], 1.0, None, ALU.add)
                dve.drain()
                nc.vector.reciprocal(beta[:], ez[:, r:r + 1])
                dve.drain()
                nc.vector.scalar_tensor_tensor(out=y[:], in0=diff[:], scalar=beta[:], in1=base[:], op0=ALU.mult,
                                               op1=ALU.add)
                dve.drain()
                nc.vector.bn_stats(stats[:], y[:])
                dve.drain()
                nc.vector.bn_aggr(mv[:, r], stats[:]).then_inc(var_ready, 1)

            def normalize(t, i):
                r = t % RING
                need(dve, rstd_ready, lin(lambda u: u, t, i))
                need(dve, y_stored[r], lin(lambda u: 16 * ((u - 1) // RING), t, i))
                nc.vector.tensor_scalar(y_out[:, r], y[:], mv[:, r, 0:1], rstd[:, r:r + 1], ALU.subtract,
                                        ALU.mult).then_inc(y_ready, 1)

            def step(t, tt, i):
                ahead = None
                if valid(t + 2):
                    ahead = dve.snap(tt + 2) if i is not None else t + 2
                if valid(t):
                    score_chunk(t, i, 0)
                if valid(t - 1):
                    attend(t - 1, i)
                if valid(t + 2):
                    scan_half(t + 2, i, 0)
                if valid(t - 1):
                    gate(t - 1, i)
                if valid(t + 2):
                    scan_half(t + 2, i, 1)
                if valid(t - 1):
                    normalize(t - 1, i)
                if valid(t + 2):
                    list_edges(t + 2, ahead, i)
                if valid(t):
                    weigh_chunk(t, i, 0)
                    for c in range(1, n_chunks(t)):
                        dve.drain()
                        score_chunk(t, i, c)
                        weigh_chunk(t, i, c)
                    if n_chunks(t) > 1:
                        join_chunks(t, i)

            dve.wait_ge(consts, CONSTS)
            program(dve, lambda t: (shape(t), shape(t + 2), shape(t - 1)), step)

            dve.drain()
            dve.wait_ge(masked, 2 * (T - 1))
            nc.vector.tensor_reduce(over[:], edges[:], AX, ALU.add)
            dve.drain()
            nc.vector.tensor_tensor(over[:], over[:], unused[:], ALU.add)
            dve.drain()
            nc.vector.tensor_tensor(over[:], over[:], caps[:], ALU.is_gt).then_inc(over_ready, 1)
            dve.wait_ge(over_summed, 1)
            nc.vector.tensor_scalar(left[:], ps_f[:], 0.0, None, ALU.is_gt)
            dve.drain()
            nc.vector.tensor_reduce(nleft[:], left[:], AX, ALU.add)
            nc.vector.tensor_tensor(left[:], left[:], order[:], ALU.mult)
            dve.drain()
            nc.vector.tensor_copy(n_dense[:], nleft[:])
            for k in range(T // 8):
                nc.vector.max(ranked[:, 8 * k:8 * k + 8], left[:])
                dve.drain()
                nc.vector.match_replace(left[:], ranked[:, 8 * k:8 * k + 8], left[:], 0.0)
                dve.drain()
            nc.vector.tensor_scalar(tile_list[:], ranked[:], -1.0, float(T), ALU.mult, ALU.add)


def dense_tiles(nc, x, adj, kv_dram, qr_dram, kt_dram, ident, gate_w, eps_col, tile_list, n_dense, out):
    SW = 1024
    SG = N // SW
    EW = 2048
    TW = 512
    TG = N // TW
    ctx = ExitStack()
    with ctx:
        def sb(name, shape, dt):
            return ctx.enter_context(nc.sbuf_tensor(name, shape, dt))

        def ps(name, shape, dt):
            return ctx.enter_context(nc.psum_tensor(name, shape, dt))

        def sem(name):
            return ctx.enter_context(nc.semaphore("d_" + name))

        kT = sb("d_kT", [P, N], F32)
        v_rows = sb("d_v", [P, T, D], F32)
        adj_in = sb("d_adj", [P, N], F32)
        pen = sb("d_pen", [P, N], BF16)
        sc = sb("d_sc", [P, 2, N], F32)
        q_in = sb("d_q", [P, D], F32)
        qT = sb("d_qT", [P, P], F32)
        o_r = sb("d_or", [P, 2 * D], F32)
        x_in = sb("d_x", [P, D], F32)
        wT = sb("d_wT", [P, 2, TW], F32)
        gmax = sb("d_gmax", [P, H, SG], F32)
        shift = sb("d_shift", [P, H], F32)
        dsum = sb("d_dsum", [P, H, N // EW], F32)
        den = sb("d_den", [P, H], F32)
        isz = sb("d_isz", [P, H], F32)
        rden = sb("d_rden", [P, H], F32)
        junk = sb("d_junk", [P, 2 * D], F32)
        z = sb("d_z", [P, 1], F32)
        ez = sb("d_ez", [P, 1], F32)
        beta = sb("d_beta", [P, 1], F32)
        diff = sb("d_diff", [P, D], F32)
        base = sb("d_base", [P, D], F32)
        y = sb("d_y", [P, D], F32)
        stats = sb("d_stats", [P, 6], F32)
        mv = sb("d_mv", [P, 2], F32)
        lnv = sb("d_lnv", [P, 1], F32)
        rstd = sb("d_rstd", [P, 1], F32)
        y_out = sb("d_yout", [P, D], F32)

        ps_s = [ps(f"d_ps_s{i}", [P, SW], F32) for i in range(2)]
        ps_w = [ps(f"d_ps_w{i}", [P, TW], F32) for i in range(2)]
        ps_q = ps("d_ps_q", [P, P], F32)
        ps_o = ps("d_ps_o", [P, D], F32)

        tables_in = sem("tables_in")
        adj_loaded = sem("adj_loaded")
        rows_loaded = sem("rows_loaded")
        pen_ready = sem("pen_ready")
        q_turned = sem("q_turned")
        qT_ready = sem("qT_ready")
        scored = sem("scored")
        masked = sem("masked")
        shift_ready = sem("shift_ready")
        expd = sem("expd")
        turned = sem("turned")
        wT_ready = sem("wT_ready")
        summed = sem("summed")
        z_ready = sem("z_ready")
        ez_ready = sem("ez_ready")
        var_ready = sem("var_ready")
        rstd_ready = sem("rstd_ready")
        y_ready = sem("y_ready")
        y_stored = sem("y_stored")
        turn = sem("turn")

        def count(eng):
            return eng.value_load(n_dense[0:1, 0:1], min_val=1, max_val=T)

        def held(eng, sem, value):
            eng.wait_ge(sem, value)
            eng.sem_inc(turn, 1)

        block = ctx.enter_context(nc.Block())

        @block.sync
        def _(sp):
            sp.dma_start(kT[:], kt_dram).then_inc(tables_in, 16)
            sp.dma_start(v_rows[:], kv_dram[:, D:2 * D].rearrange("(b p) c -> p b c", p=P)).then_inc(tables_in, 16)
            n = count(sp)
            with sp.Fori(0, n) as i:
                tile = sp.value_load(tile_list[0:1, bass.ds(i, 1)], min_val=0, max_val=T - 1)
                row = sp.snap(tile * P)
                sp.wait_ge(pen_ready, i)
                sp.dma_start(adj_in[:], adj[bass.ds(row, P), :]).then_inc(adj_loaded, 16)
                sp.wait_ge(y_ready, i)
                sp.dma_start(q_in[:], qr_dram[bass.ds(row, P), 0:D]).then_inc(rows_loaded, 16)
                sp.dma_start(o_r[:, D:2 * D], qr_dram[bass.ds(row, P), D:2 * D]).then_inc(rows_loaded, 16)
                sp.dma_start(x_in[:], x[bass.ds(row, P), :]).then_inc(rows_loaded, 16)
                sp.wait_ge(y_ready, i + 1)
                sp.dma_start(out[bass.ds(row, P), :], y_out[:]).then_inc(y_stored, 16)
                sp.wait_ge(y_stored, 16 * i + 16)
                sp.sem_inc(turn, 1)

        @block.tensor
        def _(pe):
            pe.wait_ge(tables_in, 32)
            n = count(pe)
            with pe.Fori(0, n) as i:
                pe.wait_ge(rows_loaded, 48 * i + 48)
                nc.tensor.transpose(ps_q[:], q_in[:], ident[:]).then_inc(q_turned, 1)
                pe.wait_ge(qT_ready, i + 1)

                def scores(h):
                    for g in range(SG):
                        pe.wait_ge(masked, H * SG * i + (h * SG + g - 1)) if h * SG + g >= 2 else None
                        for k in range(SW // 512):
                            col = g * SW + k * 512
                            last = nc.tensor.matmul(ps_s[g % 2][:, k * 512:(k + 1) * 512], qT[h * C:(h + 1) * C, :],
                                                    kT[h * C:(h + 1) * C, col:col + 512], start=True, stop=True)
                        last.then_inc(scored, 1)

                scores(0)
                for h in range(H):
                    if h + 1 < H:
                        scores(h + 1)
                    for g in range(TG):
                        step = TG * (H * i + h) + g
                        pe.wait_ge(expd, (N // EW) * (H * i + h) + g * TW // EW + 1)
                        for k in range(TW // P):
                            col = g * TW + k * P
                            last = nc.tensor.transpose(ps_w[g % 2][:, k * P:(k + 1) * P], sc[:, h % 2, col:col + P],
                                                       ident[:])
                        last.then_inc(turned, 1)
                        pe.wait_ge(wT_ready, step + 1)
                        for k in range(TW // P):
                            b = g * (TW // P) + k
                            last = nc.tensor.matmul(ps_o[:, h * C:(h + 1) * C], wT[:, g % 2, k * P:(k + 1) * P],
                                                    v_rows[:, b, h * C:(h + 1) * C], start=(b == 0), stop=(b == T - 1))
                        last.then_inc(summed, 1)
                pe.wait_ge(z_ready, i + 1)
                pe.sem_inc(turn, 1)

        @block.scalar
        def _(act):
            act.preload_act_table_set("natural_log_exp_and_others")
            n = count(act)
            with act.Fori(0, n) as i:
                act.wait_ge(q_turned, i + 1)
                nc.scalar.copy(qT[:], ps_q[:]).then_inc(qT_ready, 1)
                for h in range(H):
                    act.wait_ge(shift_ready, H * i + h + 1)
                    for k in range(N // EW):
                        part = sc[:, h % 2, k * EW:(k + 1) * EW]
                        nc.scalar.activation(part, part, ACT.Exp, bias=shift[:, h:h + 1], scale=SCALE,
                                             accum_out=dsum[:, h, k:k + 1]).then_inc(expd, 1)
                    for g in range(TG):
                        step = TG * (H * i + h) + g
                        act.wait_ge(turned, step + 1)
                        nc.scalar.copy(wT[:, g % 2], ps_w[g % 2][:]).then_inc(wT_ready, 1)
                act.wait_ge(z_ready, i + 1)
                nc.scalar.activation(ez[:], z[:], ACT.Exp, scale=-1.0).then_inc(ez_ready, 1)
                act.wait_ge(var_ready, i + 1)
                nc.scalar.activation(lnv[:], mv[:, 1:2], ACT.Ln, bias=eps_col[:])
                act.drain()
                nc.scalar.activation(rstd[:], lnv[:], ACT.Exp, scale=-0.5).then_inc(rstd_ready, 1)

        @block.vector
        def _(dve):
            n = count(dve)
            with dve.Fori(0, n) as i:
                dve.wait_ge(adj_loaded, 16 * i + 16)
                nc.vector.tensor_scalar(pen[:], adj_in[:], 0.0, MASKED, ALU.is_equal, ALU.mult).then_inc(pen_ready, 1)
                dve.drain()
                for h in range(H):
                    for g in range(SG):
                        held(dve, scored, H * SG * i + h * SG + g + 1)
                        if g == 0 and h >= 2:
                            held(dve, turned, TG * (H * i + h - 1))
                        nc.vector.tensor_tensor_reduce(
                            out=sc[:, h % 2, g * SW:(g + 1) * SW], in0=ps_s[g % 2][:], in1=pen[:, g * SW:(g + 1) * SW],
                            scale=1.0, scalar=FLOOR, op0=ALU.add, op1=ALU.max,
                            accum_out=gmax[:, h, g:g + 1]).then_inc(masked, 1)
                    dve.drain()
                    nc.vector.tensor_reduce(z[:], gmax[:, h], AX, ALU.max)
                    dve.drain()
                    nc.vector.tensor_scalar(shift[:, h:h + 1], z[:], -SCALE, None, ALU.mult).then_inc(shift_ready, 1)
                dve.wait_ge(expd, (N // EW) * H * (i + 1))
                nc.vector.tensor_reduce(den[:], dsum[:], AX, ALU.add)
                dve.drain()
                nc.vector.tensor_scalar(isz[:], den[:], 0.0, None, ALU.is_equal)
                dve.drain()
                nc.vector.tensor_tensor(den[:], den[:], isz[:], ALU.add)
                dve.drain()
                nc.vector.reciprocal(rden[:], den[:])
                dve.drain()
                dve.wait_ge(summed, TG * H * (i + 1))
                dve.wait_ge(rows_loaded, 48 * i + 48)
                nc.vector.tensor_tensor(o_r[:, 0:D].rearrange("p (c h) -> p h c", h=H),
                                        ps_o[:].rearrange("p (h c) -> p h c", h=H),
                                        rden[:].unsqueeze(2).to_broadcast([P, H, C]), ALU.mult)
                dve.drain()
                nc.vector.tensor_tensor_reduce(out=junk[:], in0=o_r[:], in1=gate_w[:], scale=1.0, scalar=0.0,
                                               op0=ALU.mult, op1=ALU.add, accum_out=z[:]).then_inc(z_ready, 1)
                nc.vector.tensor_tensor(diff[:], o_r[:, D:2 * D], o_r[:, 0:D], ALU.subtract)
                nc.vector.tensor_tensor(base[:], x_in[:], o_r[:, 0:D], ALU.add)
                dve.wait_ge(ez_ready, i + 1)
                nc.vector.tensor_scalar(ez[:], ez[:], 1.0, None, ALU.add)
                dve.drain()
                nc.vector.reciprocal(beta[:], ez[:])
                dve.drain()
                nc.vector.scalar_tensor_tensor(out=y[:], in0=diff[:], scalar=beta[:], in1=base[:], op0=ALU.mult,
                                               op1=ALU.add)
                dve.drain()
                nc.vector.bn_stats(stats[:], y[:])
                dve.drain()
                nc.vector.bn_aggr(mv[:], stats[:]).then_inc(var_ready, 1)
                dve.wait_ge(rstd_ready, i + 1)
                dve.wait_ge(y_stored, 16 * i)
                nc.vector.tensor_scalar(y_out[:], y[:], mv[:, 0:1], rstd[:], ALU.subtract, ALU.mult).then_inc(y_ready, 1)


_INS = ['x', 'adj', 'L0_gnn_Wq', 'L0_gnn_bq', 'L0_gnn_Wk', 'L0_gnn_bk', 'L0_gnn_Wv', 'L0_gnn_bv', 'L0_gnn_Ws',
        'L0_gnn_bs', 'L0_gnn_Wb']


def kernel(**inputs):
    import numpy as _np
    import concourse.bacc as _bacc
    from concourse import mybir as _mybir
    from concourse.bass_utils import run_bass_kernel_spmd as _run

    nc = _bacc.Bacc("TRN2", target_bir_lowering=False, num_devices=1)
    arrays, args = {}, []
    for name in _INS:
        a = _np.ascontiguousarray(inputs[name])
        arrays[f"in_{name}"] = a
        args.append(nc.dram_tensor(f"in_{name}", a.shape, _mybir.dt.from_np(a.dtype), kind="ExternalInput").ap())
    args.append(nc.dram_tensor("out_rows", (8192, 128), _mybir.dt.float32, kind="ExternalOutput").ap())
    gnn_resnorm_kernel(nc, *args)
    r = _run(nc, [arrays], core_ids=[0])
    return r.results[0]["out_rows"]
```

```python
import concourse.bass as bass
from concourse import mybir
from contextlib import ExitStack

F32 = mybir.dt.float32
BF16 = mybir.dt.bfloat16
U16 = mybir.dt.uint16
U32 = mybir.dt.uint32
I32 = mybir.dt.int32
ALU = mybir.AluOpType
ACT = mybir.ActivationFunctionType
AX = mybir.AxisListType.X

P = 128
N = 8192
D = 128
H, C = 4, 32
T = N // P
SCALE = float(C) ** -0.5
EPS = 1e-5
MASKED = -1e30
FLOOR = -1e29
TINY = 1e-30
HALF = N // 2
RING = 3
ORDER = [0, 28] + [t for k in range(1, 5) for t in (k, 18 + 2 * k, 19 + 2 * k)] \
    + [t for k in range(15) for t in (5 + k, 29 + k)] + list(range(44, T))
GROUP = 4


def gnn_resnorm_kernel(nc, x, adj, Wq, bq, Wk, bk, Wv, bv, Ws, bs, Wb, out):
    outer = ExitStack()
    with outer:
        kv_dram = nc.dram_tensor("kv_rows", (N, 2 * D), F32, kind="Internal").ap()
        qr_dram = nc.dram_tensor("qr_rows", (N, 2 * D), F32, kind="Internal").ap()
        kt_dram = nc.dram_tensor("k_columns", (D, N), F32, kind="Internal").ap()

        def keep(name, shape, dt):
            return outer.enter_context(nc.sbuf_tensor(name, shape, dt))

        ident = keep("ident", [P, P], F32)
        gate_w = keep("gate_w", [P, 2 * D], F32)
        eps_col = keep("eps_col", [P, 1], F32)
        tile_list = keep("tile_list", [1, T], I32)
        n_dense = keep("n_dense", [1, 1], I32)

        adj_in = keep("adj_in", [P, RING, HALF], F32)
        adj_loaded = [outer.enter_context(nc.semaphore(f"adj_loaded{i}")) for i in range(RING)]

        project_nodes(nc, x, Wq, bq, Wk, bk, Wv, bv, Ws, bs, Wb, kv_dram, qr_dram, kt_dram,
                      ident, gate_w, eps_col, adj, adj_in, adj_loaded)
        sparse_tiles(nc, x, adj, kv_dram, qr_dram, ident, gate_w, eps_col, tile_list, n_dense, adj_in, adj_loaded, out)
        dense_tiles(nc, x, adj, kv_dram, qr_dram, kt_dram, ident, gate_w, eps_col, tile_list, n_dense, adj_in, out)


def project_nodes(nc, x, Wq, bq, Wk, bk, Wv, bv, Ws, bs, Wb, kv_dram, qr_dram, kt_dram,
                  ident, gate_w, eps_col, adj, adj_in, adj_loaded):
    ctx = ExitStack()
    with ctx:
        def sb(name, shape, dt):
            return ctx.enter_context(nc.sbuf_tensor(name, shape, dt))

        def ps(name, shape, dt):
            return ctx.enter_context(nc.psum_tensor(name, shape, dt))

        def sem(name):
            return ctx.enter_context(nc.semaphore(name))

        w_all = sb("w_all", [P, 4 * D], F32)
        b_row = sb("b_row", [1, 4 * D], F32)
        b_all = sb("b_all", [P, 4 * D], F32)
        bk_col = sb("bk_col", [P, 1], F32)
        wb_row = sb("wb_row", [1, 3 * D], F32)
        gw_row = sb("gw_row", [1, 2 * D], F32)
        ones = sb("ones", [1, P], F32)
        x_in = sb("x_in", [P, 2, GROUP, D], F32)
        xT = sb("xT", [P, 2, GROUP * P], F32)
        rows = sb("rows", [P, 2, GROUP, 4 * D], F32)
        kT = sb("kT", [P, 2, GROUP * P], F32)
        ps_t = [ps(f"ps_t{i}", [P, GROUP * P], F32) for i in range(2)]
        ps_r = [ps(f"ps_r{i}", [P, 4 * D], F32) for i in range(4)]
        ps_k = [ps(f"ps_k{i}", [P, GROUP * P], F32) for i in range(2)]

        weights_in = sem("weights_in")
        x_loaded = [sem(f"x_loaded{i}") for i in range(2)]
        const_ready = sem("const_ready")
        bias_spread = sem("bias_spread")
        bias_ready = sem("bias_ready")
        x_turned = sem("x_turned")
        xT_ready = sem("xT_ready")
        rows_summed = sem("rows_summed")
        rows_ready = sem("rows_ready")
        kT_summed = sem("kT_summed")
        kT_ready = sem("kT_ready")
        stored = [sem(f"stored{i}") for i in range(2)]
        sp_turn = sem("sp_turn")

        def node_rows(a, row):
            return a[bass.ds(row, GROUP * P), :].rearrange("(j p) c -> p j c", p=P)

        block = ctx.enter_context(nc.Block())

        @block.sync
        def _(sp):
            for k, w in enumerate((Wk, Wv, Wq, Ws)):
                sp.dma_start(w_all[:, k * D:(k + 1) * D], w).then_inc(weights_in, 16)
            for k, b in enumerate((bk, bv, bq, bs)):
                sp.dma_start(b_row[0:1, k * D:(k + 1) * D], b.rearrange("(a c) -> a c", a=1)).then_inc(weights_in, 16)
            sp.dma_start(bk_col[:], bk.rearrange("(c a) -> c a", a=1)).then_inc(weights_in, 16)
            sp.dma_start(wb_row[:], Wb.rearrange("c a -> a c")).then_inc(weights_in, 16)
            for g in range(2):
                sp.dma_start(x_in[:, g], node_rows(x, g * GROUP * P)).then_inc(x_loaded[g], 16)
            for q in range(RING):
                row, h = ORDER[1 + q // 2] * P, q % 2
                sp.dma_start(adj_in[:, q], adj[row:row + P, h * HALF:(h + 1) * HALF]).then_inc(adj_loaded[q], 16)
            with sp.Fori(0, T // GROUP // 2) as i:
                for g in range(2):
                    row = sp.snap((2 * i + g) * (GROUP * P))
                    ahead = sp.snap(((2 * i + g + 2) % (T // GROUP)) * (GROUP * P))
                    sp.wait_ge(rows_ready, GROUP * (2 * i + g + 2))
                    sp.dma_start(node_rows(kv_dram, row), rows[:, g, :, 0:2 * D]).then_inc(stored[g], 16)
                    sp.dma_start(node_rows(qr_dram, row), rows[:, g, :, 2 * D:4 * D]).then_inc(stored[g], 16)
                    sp.wait_ge(kT_ready, 2 * i + g + 1)
                    sp.sem_inc(sp_turn, 1)
                    sp.dma_start(kt_dram[:, bass.ds(row, GROUP * P)], kT[:, g]).then_inc(stored[g], 16)
                    sp.dma_start(x_in[:, g], node_rows(x, ahead)).then_inc(x_loaded[g], 16)
            for g in range(2):
                sp.wait_ge(stored[g], 48 * (T // GROUP // 2))
                sp.wait_ge(x_loaded[g], 16 * (T // GROUP // 2 + 1))

        @block.gpsimd
        def _(pool):
            nc.gpsimd.memset(ones[:], 1.0).then_inc(const_ready, 1)
            nc.gpsimd.memset(eps_col[:], EPS).then_inc(const_ready, 1)
            nc.gpsimd.memset(ident[:], 0.0).then_inc(const_ready, 1)
            pool.wait_ge(const_ready, 3)
            nc.gpsimd.affine_select(out=ident[:], in_=ident[:], compare_op=ALU.not_equal, fill=1.0, base=0,
                                    pattern=[[-1, P]], channel_multiplier=1).then_inc(const_ready, 1)

        @block.tensor
        def _(pe):
            pe.wait_ge(weights_in, 160)
            pe.wait_ge(const_ready, 4)
            pe.wait_ge(bias_spread, 1)
            nc.tensor.matmul(ps_r[0][:], ones[:], b_row[:], start=True, stop=True)
            nc.tensor.matmul(ps_r[1][:, 0:2 * D], ones[:], gw_row[:], start=True, stop=True).then_inc(rows_summed, 1)
            pe.wait_ge(bias_ready, 1)
            with pe.Fori(0, T // GROUP // 2) as i:
                for g in range(2):
                    grp = 2 * i + g
                    pe.wait_ge(x_loaded[g], 16 * i + 16)
                    for j in range(GROUP):
                        last = nc.tensor.transpose(ps_t[g][:, j * P:(j + 1) * P], x_in[:, g, j], ident[:])
                    last.then_inc(x_turned, 1)
                    pe.wait_ge(xT_ready, grp + 1)
                    nc.tensor.matmul(ps_k[g][:], w_all[:, 0:D], xT[:, g], start=True, stop=True).then_inc(kT_summed, 1)
                    for j in range(GROUP):
                        pe.wait_ge(rows_ready, GROUP * grp + j + 1)
                        nc.tensor.matmul(ps_r[j][:], xT[:, g, j * P:(j + 1) * P], w_all[:], start=True,
                                         stop=True).then_inc(rows_summed, 1)

        @block.scalar
        def _(act):
            act.wait_ge(weights_in, 160)
            with act.Fori(0, T // GROUP // 2) as i:
                for g in range(2):
                    grp = 2 * i + g
                    act.wait_ge(x_turned, grp + 1)
                    nc.scalar.copy(xT[:, g], ps_t[g][:]).then_inc(xT_ready, 1)
                    act.wait_ge(stored[g], 48 * i)
                    act.wait_ge(kT_summed, grp + 1)
                    nc.scalar.activation(kT[:, g], ps_k[g][:], ACT.Identity, bias=bk_col[:]).then_inc(kT_ready, 1)

        @block.vector
        def _(dve):
            dve.wait_ge(weights_in, 160)
            nc.vector.tensor_tensor(gw_row[0:1, 0:D], wb_row[0:1, 0:D], wb_row[0:1, 2 * D:3 * D], ALU.add)
            nc.vector.tensor_tensor(gw_row[0:1, D:2 * D], wb_row[0:1, D:2 * D], wb_row[0:1, 2 * D:3 * D],
                                    ALU.subtract).then_inc(bias_spread, 1)
            dve.wait_ge(rows_summed, 1)
            nc.vector.tensor_copy(b_all[:], ps_r[0][:])
            nc.vector.tensor_copy(gate_w[:], ps_r[1][:, 0:2 * D]).then_inc(bias_ready, 1)
            dve.drain()
            dve.sem_inc(rows_ready, GROUP)
            with dve.Fori(0, T // GROUP // 2) as i:
                for g in range(2):
                    dve.wait_ge(stored[g], 48 * i)
                    for j in range(GROUP):
                        dve.wait_ge(rows_summed, 4 * (2 * i + g) + j + 2)
                        nc.vector.tensor_tensor(rows[:, g, j], ps_r[j][:], b_all[:], ALU.add).then_inc(rows_ready, 1)


def sparse_tiles(nc, x, adj, kv_dram, qr_dram, ident, gate_w, eps_col, tile_list, n_dense, adj_in, adj_loaded, out):
    BODY = 2 * RING
    MAX_S = 24
    ACT_S = 8
    NO_EDGE = N

    SHAPES = [(1, 4, 20, 32, 16), (2, 4, 16, 32, 16), (3, 4, 15, 32, 16), (4, 3, 17, 32, 16), (5, 2, 22, 16, 8),
              (11, 2, 17, 16, 8), (20, 1, 24, 8, 4), (29, 1, 22, 8, 4)]

    def valid(t):
        return 1 <= t < T

    def shape(t):
        return [s for s in SHAPES if s[0] <= ORDER[t]][-1][1:] if valid(t) else None

    def n_chunks(t):
        return shape(t)[0] if valid(t) else 0

    def slots(t):
        return shape(t)[1]

    def cap(t):
        return n_chunks(t) * slots(t)

    def chunks_before(t):
        return sum(n_chunks(u) for u in range(1, t))

    def multi_upto(t):
        return sum(n_chunks(u) > 1 for u in range(1, t + 1))

    def slots_landed(t, c):
        g = chunks_before(t) + c
        at, total = 0, 0
        for u in range(1, t + 1):
            for _ in range(n_chunks(u)):
                if at <= g and at % RING == g % RING:
                    total += 16 * slots(u)
                at += 1
        return total

    def runs(sign):
        def recurs(t):
            near = range(t - 1, t + 5)
            return (all(valid(u) and valid(u + BODY) for u in near) and sign(t) == sign(t + BODY)
                    and all(ORDER[u + BODY] - ORDER[u] == ORDER[u + 2 * BODY] - ORDER[u + BODY]
                            for u in near if valid(u + 2 * BODY))
                    and all(n_chunks(u) == n_chunks(u + BODY) for u in near)
                    and sum(n_chunks(t + u) for u in range(BODY)) % RING == 0)

        t, found = -2, []
        while t <= T:
            bodies = 1
            while all(t + bodies * BODY + u <= T and recurs(t + (bodies - 1) * BODY + u) for u in range(BODY)):
                bodies += 1
            found.append((t, bodies if bodies > 1 else None))
            t += BODY * bodies if bodies > 1 else 1
        return found

    def program(eng, sign, step):
        for t0, bodies in runs(sign):
            if bodies is None:
                step(t0, None)
            else:
                with eng.Fori(0, bodies) as i:
                    for u in range(BODY):
                        step(t0 + u, i)

    def lin(count, t, i):
        return count(t) if i is None else count(t) + i * (count(t + BODY) - count(t))

    def tile_at(eng, t, i, scale=1):
        return scale * ORDER[t] if i is None else eng.snap(lin(lambda u: scale * ORDER[u], t, i))

    ctx = ExitStack()
    with ctx:
        def sb(name, shape, dt):
            return ctx.enter_context(nc.sbuf_tensor("s_" + name, shape, dt))

        def sem(name):
            return ctx.enter_context(nc.semaphore("s_" + name))

        mask = sb("mask", [P, RING, HALF], BF16)
        keys = sb("keys", [P, N], U16)
        kv = sb("kv", [P, RING, MAX_S, 2 * D], F32)
        prod = sb("prod", [P, MAX_S, D], F32)
        cand = sb("cand", [P, 8 * 48], F32)
        top = sb("top", [P, 80], F32)
        empty = sb("empty", [P, RING, 80], F32)
        idx = sb("idx", [P, RING, 80], U32)
        q_in = sb("q", [P, RING, D], F32)
        o_r = sb("or", [P, RING, 2 * D], F32)
        x_in = sb("x", [P, RING, D], F32)
        raw = sb("raw", [P, MAX_S * H], F32)
        sc = sb("sc", [P, (1 + MAX_S) * H], F32)
        e = sb("e", [P, MAX_S * H], F32)
        peak = sb("peak", [P, RING, 4, H], F32)
        dens = sb("dens", [P, RING, 4, H], F32)
        below = sb("below", [P, RING, 4, H], F32)
        share = sb("share", [P, RING, 4, H], F32)
        mtop = sb("mtop", [P, H], F32)
        parts = sb("parts", [P, 4, D], F32)
        osum = sb("osum", [P, D], F32)
        dtmp = sb("dtmp", [P, 4, H], F32)
        den = sb("den", [P, H], F32)
        divisor = sb("divisor", [P, H], F32)
        rden = sb("rden", [P, H], F32)
        junk = sb("junk", [P, 2 * D], F32)
        z = sb("z", [P, RING], F32)
        ez = sb("ez", [P, RING], F32)
        beta = sb("beta", [P, 1], F32)
        diff = sb("diff", [P, D], F32)
        base = sb("base", [P, D], F32)
        y = sb("y", [P, D], F32)
        stats = sb("stats", [P, 6], F32)
        mv = sb("mv", [P, RING, 2], F32)
        lnv = sb("lnv", [P, 1], F32)
        rstd = sb("rstd", [P, RING], F32)
        y_out = sb("yout", [P, RING, D], F32)
        edges = sb("edges", [P, T, 2], F32)
        unused = sb("unused", [P, T], F32)
        caps = sb("caps", [P, T], F32)
        over = sb("over", [P, T], F32)
        ones = sb("ones", [P, 1], F32)
        order = sb("order", [1, T], F32)
        left = sb("left", [1, T], F32)
        ranked = sb("ranked", [1, T], F32)
        nleft = sb("nleft", [1, 1], F32)

        acc = [ctx.enter_context(nc.psum_tensor(f"s_acc{i}", [P, 4, D], F32)) for i in range(RING)]
        ps_f = ctx.enter_context(nc.psum_tensor("s_ps_f", [1, T], F32))

        consts = sem("consts")
        adj_used = sem("adj_used")
        masked = sem("masked")
        scanned = sem("scanned")
        idx_ready = sem("idx_ready")
        gathered = [sem(f"gathered{i}") for i in range(RING)]
        rows_loaded = [sem(f"rows_loaded{i}") for i in range(RING)]
        shifted = sem("shifted")
        expd = sem("expd")
        weighted = sem("weighted")
        act_weighted = sem("act_weighted")
        summed = sem("summed")
        below_ready = sem("below_ready")
        share_ready = sem("share_ready")
        z_ready = sem("z_ready")
        ez_ready = sem("ez_ready")
        var_ready = sem("var_ready")
        rstd_ready = sem("rstd_ready")
        y_ready = sem("y_ready")
        y_stored = [sem(f"y_stored{i}") for i in range(RING)]
        over_ready = sem("over_ready")
        over_summed = sem("over_summed")
        turn = sem("turn")

        def need(eng, sem, value, carry=False):
            if isinstance(value, int) and value <= 0:
                return
            eng.wait_ge(sem, value)
            if carry:
                eng.sem_inc(turn, 1)

        def half_no(t, i, h):
            return lin(lambda u: 2 * (u - 1) + h + 1, t, i)

        def chunk_no(t, i, c):
            return lin(lambda u: chunks_before(u) + c + 1, t, i)

        def half_slot(t, h):
            return (2 * (t - 1) + h) % RING

        def kv_slot(t, c):
            return (chunks_before(t) + c) % RING

        CONSTS = 8 + len(SHAPES)
        block = ctx.enter_context(nc.Block())

        @block.sync
        def _(sp):
            def step(t, i):
                for h in range(2):
                    if valid(t + 4):
                        row = tile_at(sp, t + 4, i, P)
                        if i is None and 2 * (t + 3) + h < RING:
                            continue
                        need(sp, adj_used, half_no(t + 4, i, h) - RING, i is not None)
                        sp.dma_start(adj_in[:, half_slot(t + 4, h)],
                                     adj[bass.ds(row, P), h * HALF:(h + 1) * HALF]
                                     ).then_inc(adj_loaded[half_slot(t + 4, h)], 16)
                if valid(t - 1):
                    row = tile_at(sp, t - 1, i, P)
                    need(sp, y_ready, lin(lambda u: u - 1, t, i), i is not None)
                    sp.dma_start(out[bass.ds(row, P), :], y_out[:, (t - 1) % RING]).then_inc(y_stored[(t - 1) % RING], 16)
                if valid(t + 2):
                    r = (t + 2) % RING
                    row = tile_at(sp, t + 2, i, P)
                    sp.dma_start(q_in[:, r], qr_dram[bass.ds(row, P), 0:D]).then_inc(rows_loaded[r], 16)
                    sp.dma_start(o_r[:, r, D:2 * D], qr_dram[bass.ds(row, P), D:2 * D]).then_inc(rows_loaded[r], 16)
                    sp.dma_start(x_in[:, r], x[bass.ds(row, P), :]).then_inc(rows_loaded[r], 16)

            program(sp, lambda t: (valid(t + 4), valid(t - 1), valid(t + 2)), step)
            for r in range(RING):
                sp.wait_ge(y_stored[r], 16 * sum(t % RING == r for t in range(1, T)))

        @block.gpsimd
        def _(pool):
            nc.gpsimd.iota(keys[:], pattern=[[-1, N]], base=N, channel_multiplier=0).then_inc(consts, 1)
            nc.gpsimd.iota(order[:], pattern=[[-1, T]], base=T, channel_multiplier=0,
                           allow_small_or_imprecise_dtypes=True).then_inc(consts, 1)
            nc.gpsimd.memset(kv[:], 0.0).then_inc(consts, 1)
            nc.gpsimd.memset(edges[:, 0], 0.0).then_inc(consts, 1)
            nc.gpsimd.memset(unused[:, 0:1], 0.0).then_inc(consts, 1)
            nc.gpsimd.memset(caps[:, 0:1], -1.0).then_inc(consts, 1)
            for k, s in enumerate(SHAPES):
                end = SHAPES[k + 1][0] if k + 1 < len(SHAPES) else T
                nc.gpsimd.memset(caps[:, s[0]:end], float(s[1] * s[2])).then_inc(consts, 1)
            nc.gpsimd.memset(ones[:], 1.0).then_inc(consts, 1)
            nc.gpsimd.memset(sc[:, 0:H], FLOOR).then_inc(consts, 1)
            pool.wait_ge(consts, CONSTS)
            last_node = pool.to_reg(N - 1)

            def step(t, i):
                if not valid(t):
                    return
                need(pool, idx_ready, lin(lambda u: u, t, i), True)
                for c in range(n_chunks(t)):
                    need(pool, summed, lin(lambda u: chunks_before(u) + c + 1 - RING, t, i), True)
                    for s in range(slots(t)):
                        col = c * slots(t) + s
                        nc.gpsimd.indirect_dma_start(
                            out=kv[:, kv_slot(t, c), s], out_offset=None, in_=kv_dram[:, :],
                            in_offset=bass.IndirectOffsetOnAxis(ap=idx[:, t % RING, col:col + 1], axis=0),
                            bounds_check=last_node, oob_is_err=False).then_inc(gathered[kv_slot(t, c)], 16)

            program(pool, lambda t: shape(t), step)

        @block.tensor
        def _(pe):
            def step(t, i):
                if not valid(t):
                    return
                for c in range(n_chunks(t)):
                    need(pe, weighted, chunk_no(t, i, c))
                    if c == 0:
                        need(pe, act_weighted, lin(lambda u: u, t, i))
                    for s in range(slots(t)):
                        last = nc.tensor.matmul(acc[t % RING][:, c], ident[:], kv[:, kv_slot(t, c), s, D:2 * D],
                                                start=(s == 0), stop=(s == slots(t) - 1))
                    last.then_inc(summed, 1)

            program(pe, lambda t: shape(t), step)
            pe.wait_ge(over_ready, 1)
            nc.tensor.matmul(ps_f[:], ones[:], over[:], start=True, stop=True).then_inc(over_summed, 1)

        @block.scalar
        def _(act):
            act.preload_act_table_set("natural_log_exp_and_others")

            def exp_chunk(t, i, c):
                need(act, shifted, chunk_no(t, i, c))
                w = slots(t) * H
                nc.scalar.activation(e[:, 0:w], sc[:, H:H + w], ACT.Exp, scale=SCALE).then_inc(expd, 1)

            def mask_half(t, tt, i, h):
                b = half_slot(t, h)
                need(act, adj_loaded[b], lin(lambda u: 16 * ((2 * (u - 1) + h) // RING + 1), t, i))
                need(act, scanned, half_no(t, i, h) - RING)
                nc.scalar.activation(mask[:, b], adj_in[:, b], ACT.Sign).then_inc(adj_used, 1)
                act.drain()
                nc.scalar.activation(mask[:, b], mask[:, b], ACT.Square,
                                     accum_out=edges[:, bass.ds(tt, 1), h]).then_inc(masked, 1)

            def step(t, i):
                if valid(t):
                    exp_chunk(t, i, 0)
                if valid(t - 1):
                    r = (t - 1) % RING
                    need(act, z_ready, lin(lambda u: u - 1, t, i))
                    nc.scalar.activation(ez[:, r:r + 1], z[:, r:r + 1], ACT.Exp, scale=-1.0).then_inc(ez_ready, 1)
                if valid(t):
                    need(act, expd, chunk_no(t, i, 0))
                    for s in range(slots(t) - ACT_S, slots(t)):
                        for h in range(H):
                            v = kv[:, kv_slot(t, 0), s, D + h * C:D + (h + 1) * C]
                            last = nc.scalar.activation(v, v, ACT.Copy, scale=e[:, s * H + h:s * H + h + 1])
                    last.then_inc(act_weighted, 1)
                ahead = None
                if valid(t + 3):
                    ahead = tile_at(act, t + 3, i)
                    mask_half(t + 3, ahead, i, 0)
                if valid(t - 1):
                    r = (t - 1) % RING
                    need(act, var_ready, lin(lambda u: u - 1, t, i))
                    nc.scalar.activation(lnv[:], mv[:, r, 1:2], ACT.Ln, bias=eps_col[:])
                    act.drain()
                    nc.scalar.activation(rstd[:, r:r + 1], lnv[:], ACT.Exp, scale=-0.5).then_inc(rstd_ready, 1)
                if n_chunks(t) > 1:
                    exp_chunk(t, i, 1)
                if valid(t + 3):
                    mask_half(t + 3, ahead, i, 1)
                if valid(t):
                    for c in range(2, n_chunks(t)):
                        exp_chunk(t, i, c)
                    if n_chunks(t) > 1:
                        r = t % RING
                        need(act, below_ready, lin(multi_upto, t, i))
                        nc.scalar.activation(share[:, r, 0:n_chunks(t)], below[:, r, 0:n_chunks(t)], ACT.Exp,
                                             scale=SCALE).then_inc(share_ready, 1)

            program(act, lambda t: (shape(t), n_chunks(t - 1), valid(t + 3), valid(t - 1)), step)

        @block.vector
        def _(dve):
            def score_chunk(t, i, c):
                r, b, s = t % RING, kv_slot(t, c), slots(t)
                if c == 0:
                    need(dve, rows_loaded[r], lin(lambda u: 48 * ((u - 1) // RING + 1), t, i))
                need(dve, gathered[b], lin(lambda u: slots_landed(u, c), t, i))
                nc.vector.tensor_tensor(prod[:, 0:s], kv[:, b, 0:s, 0:D],
                                        q_in[:, r].unsqueeze(1).to_broadcast([P, s, D]), ALU.mult)
                dve.drain()
                nc.vector.tensor_reduce(raw[:, 0:s * H], prod[:, 0:s].rearrange("p s (h c) -> p (s h) c", h=H), AX,
                                        ALU.add)
                dve.drain()
                sc_sh = sc[:, H:(1 + s) * H].rearrange("p (s h) -> p s h", h=H)
                nc.vector.scalar_tensor_tensor(
                    out=sc_sh, in0=empty[:, r, c * s:(c + 1) * s].unsqueeze(2).to_broadcast([P, s, H]), scalar=MASKED,
                    in1=raw[:, 0:s * H].rearrange("p (s h) -> p s h", h=H), op0=ALU.mult, op1=ALU.add)
                dve.drain()
                nc.vector.tensor_reduce(peak[:, r, c], sc[:, 0:(1 + s) * H].rearrange("p (s h) -> p h s", h=H), AX,
                                        ALU.max)
                dve.drain()
                nc.vector.tensor_tensor(sc_sh, sc_sh, peak[:, r, c].unsqueeze(1).to_broadcast([P, s, H]),
                                        ALU.subtract).then_inc(shifted, 1)

            def weigh_chunk(t, i, c):
                r, b, s = t % RING, kv_slot(t, c), slots(t)
                need(dve, expd, chunk_no(t, i, c))
                own = s - ACT_S if c == 0 else s
                v = kv[:, b, 0:own, D:2 * D].rearrange("p s (h c) -> p s h c", h=H)
                e_sh = e[:, 0:own * H].rearrange("p (s h) -> p s h", h=H)
                nc.vector.tensor_tensor(v, v, e_sh.unsqueeze(3).to_broadcast([P, own, H, C]), ALU.mult).then_inc(weighted, 1)
                nc.vector.tensor_reduce(dens[:, r, c], e[:, 0:s * H].rearrange("p (s h) -> p h s", h=H), AX, ALU.add)

            def scan_half(t, i, h):
                b = half_slot(t, h)
                n_seg = shape(t)[2 + h]
                first = shape(t)[2] * h
                need(dve, masked, half_no(t, i, h))
                key = mask[:, b].bitcast(U16)
                nc.vector.tensor_tensor(key, mask[:, b], keys[:, h * HALF:(h + 1) * HALF], ALU.mult)
                dve.drain()
                seg = key.rearrange("p (j s) -> p s j", s=n_seg)
                for s in range(n_seg):
                    last = nc.vector.max(cand[:, 8 * (first + s):8 * (first + s + 1)], seg[:, s])
                last.then_inc(scanned, 1)

            def list_edges(t, tt, i):
                r = t % RING
                width = 8 * (shape(t)[2] + shape(t)[3])
                rounds = -(-cap(t) // 8)
                dve.drain()
                for k in range(rounds):
                    nc.vector.max(top[:, 8 * k:8 * k + 8], cand[:, 0:width])
                    dve.drain()
                    if k + 1 < rounds:
                        nc.vector.match_replace(cand[:, 0:width], top[:, 8 * k:8 * k + 8], cand[:, 0:width], 0.0)
                        dve.drain()
                nc.vector.tensor_scalar(idx[:, r, 0:cap(t)], top[:, 0:cap(t)], -1.0, float(NO_EDGE), ALU.mult,
                                        ALU.add).then_inc(idx_ready, 1)
                nc.vector.tensor_scalar(empty[:, r, 0:cap(t)], top[:, 0:cap(t)], 0.0, None, ALU.is_equal)
                dve.drain()
                nc.vector.tensor_reduce(unused[:, bass.ds(tt, 1)], empty[:, r, 0:cap(t)], AX, ALU.add)

            def join_chunks(t, i):
                r, n = t % RING, n_chunks(t)
                nc.vector.tensor_reduce(mtop[:], peak[:, r, 0:n].rearrange("p n h -> p h n"), AX, ALU.max)
                dve.drain()
                nc.vector.tensor_tensor(below[:, r, 0:n], peak[:, r, 0:n], mtop[:].unsqueeze(1).to_broadcast([P, n, H]),
                                        ALU.subtract).then_inc(below_ready, 1)

            def attend(t, i):
                r, n = t % RING, n_chunks(t)
                sums, total = acc[r][:, 0], dens[:, r, 0]
                dve.drain()
                need(dve, summed, lin(lambda u: chunks_before(u + 1), t, i))
                if n > 1:
                    need(dve, share_ready, lin(multi_upto, t, i))
                    w = share[:, r, 0:n]
                    nc.vector.tensor_tensor(parts[:, 0:n].rearrange("p n (h c) -> p (n h) c", h=H),
                                            acc[r][:, 0:n].rearrange("p n (h c) -> p (n h) c", h=H),
                                            w.rearrange("p n h -> p (n h)").unsqueeze(2).to_broadcast([P, n * H, C]),
                                            ALU.mult)
                    nc.vector.tensor_tensor(dtmp[:, 0:n], dens[:, r, 0:n], w, ALU.mult)
                    dve.drain()
                    nc.vector.tensor_reduce(osum[:], parts[:, 0:n].rearrange("p n c -> p c n"), AX, ALU.add)
                    nc.vector.tensor_reduce(den[:], dtmp[:, 0:n].rearrange("p n h -> p h n"), AX, ALU.add)
                    dve.drain()
                    sums, total = osum[:], den[:]
                nc.vector.tensor_scalar(divisor[:], total, TINY, None, ALU.max)
                dve.drain()
                nc.vector.reciprocal(rden[:], divisor[:])
                dve.drain()
                nc.vector.tensor_tensor(o_r[:, r, 0:D].rearrange("p (c h) -> p h c", h=H),
                                        sums.rearrange("p (h c) -> p h c", h=H),
                                        rden[:].unsqueeze(2).to_broadcast([P, H, C]), ALU.mult)
                dve.drain()
                nc.vector.tensor_tensor_reduce(out=junk[:], in0=o_r[:, r], in1=gate_w[:], scale=1.0, scalar=0.0,
                                               op0=ALU.mult, op1=ALU.add, accum_out=z[:, r:r + 1]).then_inc(z_ready, 1)
                nc.vector.tensor_tensor(diff[:], o_r[:, r, D:2 * D], o_r[:, r, 0:D], ALU.subtract)
                nc.vector.tensor_tensor(base[:], x_in[:, r], o_r[:, r, 0:D], ALU.add)

            def gate(t, i):
                r = t % RING
                need(dve, ez_ready, lin(lambda u: u, t, i))
                nc.vector.tensor_scalar(ez[:, r:r + 1], ez[:, r:r + 1], 1.0, None, ALU.add)
                dve.drain()
                nc.vector.reciprocal(beta[:], ez[:, r:r + 1])
                dve.drain()
                nc.vector.scalar_tensor_tensor(out=y[:], in0=diff[:], scalar=beta[:], in1=base[:], op0=ALU.mult,
                                               op1=ALU.add)
                dve.drain()
                nc.vector.bn_stats(stats[:], y[:])
                dve.drain()
                nc.vector.bn_aggr(mv[:, r], stats[:]).then_inc(var_ready, 1)

            def normalize(t, i):
                r = t % RING
                need(dve, rstd_ready, lin(lambda u: u, t, i))
                need(dve, y_stored[r], lin(lambda u: 16 * ((u - 1) // RING), t, i))
                nc.vector.tensor_scalar(y_out[:, r], y[:], mv[:, r, 0:1], rstd[:, r:r + 1], ALU.subtract,
                                        ALU.mult).then_inc(y_ready, 1)

            def step(t, i):
                ahead = None
                if valid(t + 2):
                    ahead = tile_at(dve, t + 2, i)
                def next_chunk(c):
                    if c < n_chunks(t):
                        weigh_chunk(t, i, c)
                    if c + 1 < n_chunks(t):
                        dve.drain()
                        score_chunk(t, i, c + 1)

                if valid(t):
                    score_chunk(t, i, 0)
                if valid(t - 1):
                    attend(t - 1, i)
                if valid(t + 2):
                    scan_half(t + 2, i, 0)
                if valid(t - 1):
                    gate(t - 1, i)
                next_chunk(0)
                if valid(t + 2):
                    scan_half(t + 2, i, 1)
                if valid(t - 1):
                    normalize(t - 1, i)
                next_chunk(1)
                if valid(t + 2):
                    list_edges(t + 2, ahead, i)
                next_chunk(2)
                next_chunk(3)
                if valid(t):
                    if n_chunks(t) > 1:
                        join_chunks(t, i)

            dve.wait_ge(consts, CONSTS)
            program(dve, lambda t: (shape(t), shape(t + 2), shape(t - 1)), step)

            dve.drain()
            dve.wait_ge(masked, 2 * (T - 1))
            nc.vector.tensor_reduce(over[:], edges[:], AX, ALU.add)
            dve.drain()
            nc.vector.tensor_tensor(over[:], over[:], unused[:], ALU.add)
            dve.drain()
            nc.vector.tensor_tensor(over[:], over[:], caps[:], ALU.is_gt).then_inc(over_ready, 1)
            dve.wait_ge(over_summed, 1)
            nc.vector.tensor_scalar(left[:], ps_f[:], 0.0, None, ALU.is_gt)
            dve.drain()
            nc.vector.tensor_reduce(nleft[:], left[:], AX, ALU.add)
            nc.vector.tensor_tensor(left[:], left[:], order[:], ALU.mult)
            dve.drain()
            nc.vector.tensor_copy(n_dense[:], nleft[:])
            for k in range(T // 8):
                nc.vector.max(ranked[:, 8 * k:8 * k + 8], left[:])
                dve.drain()
                nc.vector.match_replace(left[:], ranked[:, 8 * k:8 * k + 8], left[:], 0.0)
                dve.drain()
            nc.vector.tensor_scalar(tile_list[:], ranked[:], -1.0, float(T), ALU.mult, ALU.add)


def dense_tiles(nc, x, adj, kv_dram, qr_dram, kt_dram, ident, gate_w, eps_col, tile_list, n_dense, adj_halves, out):
    SW = 1024
    SG = N // SW
    EW = 2048
    TW = 512
    TG = N // TW
    ctx = ExitStack()
    with ctx:
        def sb(name, shape, dt):
            return ctx.enter_context(nc.sbuf_tensor(name, shape, dt))

        def ps(name, shape, dt):
            return ctx.enter_context(nc.psum_tensor(name, shape, dt))

        def sem(name):
            return ctx.enter_context(nc.semaphore("d_" + name))

        kT = sb("d_kT", [P, N], F32)
        v_rows = sb("d_v", [P, T, D], F32)
        adj_in = adj_halves[:, 0:2].rearrange("p a b -> p (a b)")
        pen = sb("d_pen", [P, N], BF16)
        sc = sb("d_sc", [P, 2, N], F32)
        q_in = sb("d_q", [P, D], F32)
        qT = sb("d_qT", [P, P], F32)
        o_r = sb("d_or", [P, 2 * D], F32)
        x_in = sb("d_x", [P, D], F32)
        wT = sb("d_wT", [P, 2, TW], F32)
        gmax = sb("d_gmax", [P, H, SG], F32)
        shift = sb("d_shift", [P, H], F32)
        dsum = sb("d_dsum", [P, H, N // EW], F32)
        den = sb("d_den", [P, H], F32)
        isz = sb("d_isz", [P, H], F32)
        rden = sb("d_rden", [P, H], F32)
        junk = sb("d_junk", [P, 2 * D], F32)
        z = sb("d_z", [P, 1], F32)
        ez = sb("d_ez", [P, 1], F32)
        beta = sb("d_beta", [P, 1], F32)
        diff = sb("d_diff", [P, D], F32)
        base = sb("d_base", [P, D], F32)
        y = sb("d_y", [P, D], F32)
        stats = sb("d_stats", [P, 6], F32)
        mv = sb("d_mv", [P, 2], F32)
        lnv = sb("d_lnv", [P, 1], F32)
        rstd = sb("d_rstd", [P, 1], F32)
        y_out = sb("d_yout", [P, D], F32)

        ps_s = [ps(f"d_ps_s{i}", [P, SW], F32) for i in range(2)]
        ps_w = [ps(f"d_ps_w{i}", [P, TW], F32) for i in range(2)]
        ps_q = ps("d_ps_q", [P, P], F32)
        ps_o = ps("d_ps_o", [P, D], F32)

        tables_in = sem("tables_in")
        v_in = sem("v_in")
        adj_loaded = sem("adj_loaded")
        rows_loaded = sem("rows_loaded")
        pen_ready = sem("pen_ready")
        q_turned = sem("q_turned")
        qT_ready = sem("qT_ready")
        scored = sem("scored")
        masked = sem("masked")
        shift_ready = sem("shift_ready")
        expd = sem("expd")
        turned = sem("turned")
        wT_ready = sem("wT_ready")
        summed = sem("summed")
        z_ready = sem("z_ready")
        ez_ready = sem("ez_ready")
        var_ready = sem("var_ready")
        rstd_ready = sem("rstd_ready")
        y_ready = sem("y_ready")
        y_stored = sem("y_stored")
        turn = sem("turn")

        def count(eng):
            return eng.value_load(n_dense[0:1, 0:1], min_val=1, max_val=T)

        def held(eng, sem, value):
            eng.wait_ge(sem, value)
            eng.sem_inc(turn, 1)

        block = ctx.enter_context(nc.Block())

        @block.sync
        def _(sp):
            sp.dma_start(kT[:], kt_dram).then_inc(tables_in, 16)
            n = count(sp)
            with sp.Fori(0, n) as i:
                tile = sp.value_load(tile_list[0:1, bass.ds(i, 1)], min_val=0, max_val=T - 1)
                row = sp.snap(tile * P)
                sp.wait_ge(pen_ready, i)
                sp.dma_start(adj_in[:], adj[bass.ds(row, P), :]).then_inc(adj_loaded, 16)
                sp.wait_ge(y_ready, i)
                sp.dma_start(q_in[:], qr_dram[bass.ds(row, P), 0:D]).then_inc(rows_loaded, 16)
                sp.dma_start(o_r[:, D:2 * D], qr_dram[bass.ds(row, P), D:2 * D]).then_inc(rows_loaded, 16)
                sp.dma_start(x_in[:], x[bass.ds(row, P), :]).then_inc(rows_loaded, 16)
                sp.wait_ge(y_ready, i + 1)
                sp.dma_start(out[bass.ds(row, P), :], y_out[:]).then_inc(y_stored, 16)
                sp.wait_ge(y_stored, 16 * i + 16)
                sp.sem_inc(turn, 1)

        @block.tensor
        def _(pe):
            pe.wait_ge(tables_in, 16)
            n = count(pe)
            with pe.Fori(0, n) as i:
                pe.wait_ge(rows_loaded, 48 * i + 48)
                nc.tensor.transpose(ps_q[:], q_in[:], ident[:]).then_inc(q_turned, 1)
                pe.wait_ge(qT_ready, i + 1)

                def scores(h):
                    for g in range(SG):
                        if h * SG + g >= 2:
                            pe.wait_ge(masked, H * SG * i + (h * SG + g - 1))
                        for k in range(SW // 512):
                            col = g * SW + k * 512
                            last = nc.tensor.matmul(ps_s[g % 2][:, k * 512:(k + 1) * 512], qT[h * C:(h + 1) * C, :],
                                                    kT[h * C:(h + 1) * C, col:col + 512], start=True, stop=True)
                        last.then_inc(scored, 1)

                scores(0)
                for h in range(H):
                    if h + 1 < H:
                        scores(h + 1)
                    if h == 0:
                        pe.wait_ge(v_in, 16)
                    for g in range(TG + 1):
                        step = TG * (H * i + h) + g
                        if g < TG:
                            pe.wait_ge(expd, (N // EW) * (H * i + h) + g * TW // EW + 1)
                            for k in range(TW // P):
                                col = g * TW + k * P
                                last = nc.tensor.transpose(ps_w[g % 2][:, k * P:(k + 1) * P],
                                                           sc[:, h % 2, col:col + P], ident[:])
                            last.then_inc(turned, 1)
                        if g > 0:
                            pe.wait_ge(wT_ready, step)
                            for k in range(TW // P):
                                b = (g - 1) * (TW // P) + k
                                last = nc.tensor.matmul(ps_o[:, h * C:(h + 1) * C],
                                                        wT[:, (g - 1) % 2, k * P:(k + 1) * P],
                                                        v_rows[:, b, h * C:(h + 1) * C], start=(b == 0),
                                                        stop=(b == T - 1))
                            last.then_inc(summed, 1)
                pe.wait_ge(z_ready, i + 1)
                pe.sem_inc(turn, 1)

        @block.scalar
        def _(act):
            act.preload_act_table_set("natural_log_exp_and_others")
            act.wait_ge(adj_loaded, 16)
            act.dma_start(v_rows[:], kv_dram[:, D:2 * D].rearrange("(b p) c -> p b c", p=P)).then_inc(v_in, 16)
            n = count(act)
            with act.Fori(0, n) as i:
                act.wait_ge(q_turned, i + 1)
                nc.scalar.copy(qT[:], ps_q[:]).then_inc(qT_ready, 1)
                for h in range(H):
                    act.wait_ge(shift_ready, H * i + h + 1)
                    for k in range(N // EW):
                        part = sc[:, h % 2, k * EW:(k + 1) * EW]
                        nc.scalar.activation(part, part, ACT.Exp, bias=shift[:, h:h + 1], scale=SCALE,
                                             accum_out=dsum[:, h, k:k + 1]).then_inc(expd, 1)
                    for g in range(TG):
                        step = TG * (H * i + h) + g
                        act.wait_ge(turned, step + 1)
                        if h or g >= 2:
                            act.wait_ge(summed, step - 1)
                        nc.scalar.copy(wT[:, g % 2], ps_w[g % 2][:]).then_inc(wT_ready, 1)
                act.wait_ge(z_ready, i + 1)
                nc.scalar.activation(ez[:], z[:], ACT.Exp, scale=-1.0).then_inc(ez_ready, 1)
                act.wait_ge(var_ready, i + 1)
                nc.scalar.activation(lnv[:], mv[:, 1:2], ACT.Ln, bias=eps_col[:])
                act.drain()
                nc.scalar.activation(rstd[:], lnv[:], ACT.Exp, scale=-0.5).then_inc(rstd_ready, 1)

        @block.vector
        def _(dve):
            n = count(dve)
            with dve.Fori(0, n) as i:
                dve.wait_ge(adj_loaded, 16 * i + 16)
                nc.vector.tensor_scalar(pen[:], adj_in[:], 0.0, MASKED, ALU.is_equal, ALU.mult).then_inc(pen_ready, 1)
                dve.drain()
                for h in range(H):
                    for g in range(SG):
                        held(dve, scored, H * SG * i + h * SG + g + 1)
                        if g == 0 and h >= 2:
                            held(dve, turned, TG * (H * i + h - 1))
                        nc.vector.tensor_tensor_reduce(
                            out=sc[:, h % 2, g * SW:(g + 1) * SW], in0=ps_s[g % 2][:], in1=pen[:, g * SW:(g + 1) * SW],
                            scale=1.0, scalar=FLOOR, op0=ALU.add, op1=ALU.max,
                            accum_out=gmax[:, h, g:g + 1]).then_inc(masked, 1)
                    dve.drain()
                    nc.vector.tensor_reduce(z[:], gmax[:, h], AX, ALU.max)
                    dve.drain()
                    nc.vector.tensor_scalar(shift[:, h:h + 1], z[:], -SCALE, None, ALU.mult).then_inc(shift_ready, 1)
                dve.wait_ge(expd, (N // EW) * H * (i + 1))
                nc.vector.tensor_reduce(den[:], dsum[:], AX, ALU.add)
                dve.drain()
                nc.vector.tensor_scalar(isz[:], den[:], 0.0, None, ALU.is_equal)
                dve.drain()
                nc.vector.tensor_tensor(den[:], den[:], isz[:], ALU.add)
                dve.drain()
                nc.vector.reciprocal(rden[:], den[:])
                dve.drain()
                dve.wait_ge(summed, TG * H * (i + 1))
                dve.wait_ge(rows_loaded, 48 * i + 48)
                nc.vector.tensor_tensor(o_r[:, 0:D].rearrange("p (c h) -> p h c", h=H),
                                        ps_o[:].rearrange("p (h c) -> p h c", h=H),
                                        rden[:].unsqueeze(2).to_broadcast([P, H, C]), ALU.mult)
                dve.drain()
                nc.vector.tensor_tensor_reduce(out=junk[:], in0=o_r[:], in1=gate_w[:], scale=1.0, scalar=0.0,
                                               op0=ALU.mult, op1=ALU.add, accum_out=z[:]).then_inc(z_ready, 1)
                nc.vector.tensor_tensor(diff[:], o_r[:, D:2 * D], o_r[:, 0:D], ALU.subtract)
                nc.vector.tensor_tensor(base[:], x_in[:], o_r[:, 0:D], ALU.add)
                dve.wait_ge(ez_ready, i + 1)
                nc.vector.tensor_scalar(ez[:], ez[:], 1.0, None, ALU.add)
                dve.drain()
                nc.vector.reciprocal(beta[:], ez[:])
                dve.drain()
                nc.vector.scalar_tensor_tensor(out=y[:], in0=diff[:], scalar=beta[:], in1=base[:], op0=ALU.mult,
                                               op1=ALU.add)
                dve.drain()
                nc.vector.bn_stats(stats[:], y[:])
                dve.drain()
                nc.vector.bn_aggr(mv[:], stats[:]).then_inc(var_ready, 1)
                dve.wait_ge(rstd_ready, i + 1)
                dve.wait_ge(y_stored, 16 * i)
                nc.vector.tensor_scalar(y_out[:], y[:], mv[:, 0:1], rstd[:], ALU.subtract, ALU.mult).then_inc(y_ready, 1)


_INS = ['x', 'adj', 'L0_gnn_Wq', 'L0_gnn_bq', 'L0_gnn_Wk', 'L0_gnn_bk', 'L0_gnn_Wv', 'L0_gnn_bv', 'L0_gnn_Ws',
        'L0_gnn_bs', 'L0_gnn_Wb']


def kernel(**inputs):
    import numpy as _np
    import concourse.bacc as _bacc
    from concourse import mybir as _mybir
    from concourse.bass_utils import run_bass_kernel_spmd as _run

    nc = _bacc.Bacc("TRN2", target_bir_lowering=False, num_devices=1)
    arrays, args = {}, []
    for name in _INS:
        a = _np.ascontiguousarray(inputs[name])
        arrays[f"in_{name}"] = a
        args.append(nc.dram_tensor(f"in_{name}", a.shape, _mybir.dt.from_np(a.dtype), kind="ExternalInput").ap())
    args.append(nc.dram_tensor("out_rows", (8192, 128), _mybir.dt.float32, kind="ExternalOutput").ap())
    gnn_resnorm_kernel(nc, *args)
    r = _run(nc, [arrays], core_ids=[0])
    return r.results[0]["out_rows"]
```
